# Optimizing a Trainium2 kernel written in Bass

```python
import numpy as np
import jax
import jax.numpy as jnp

def _softmax(x, axis=-1):
    return jax.nn.softmax(x, axis=axis)

def _gelu(x):
    return jax.nn.gelu(x, approximate=True)

def _silu(x):
    return jax.nn.silu(x)

def _sigmoid(x):
    return jax.nn.sigmoid(x)

def _layernorm(x, axis=-1, eps=1e-05):
    m = jnp.mean(x, axis=axis, keepdims=True)
    v = jnp.var(x, axis=axis, keepdims=True)
    return (x - m) / jnp.sqrt(v + eps)

def _scatter_add(tgt, idx, src, axis=0):
    return tgt.at[idx].add(src)

def _segment_sum(src, seg, n):
    return jax.ops.segment_sum(src, seg, n)
kernel_name = 'mk_prb_d1_jaxref_r4_970e04'

def setup_inputs(seed: int=0):
    np.random.seed(seed)
    _w = jnp.asarray

    def _L0_attn_setup():
        import jax, jax.numpy as jnp
        import numpy as np
        H = 16
        EPS = 1e-06
        key = jax.random.key(seed)
        ks = jax.random.split(key, 5)
        B, N, D = (4, 1024, 256)
        x = jax.random.normal(ks[0], (B, N, D), dtype=jnp.float32)
        q = jax.random.normal(ks[1], (D,), dtype=jnp.float32)
        k = jax.random.normal(ks[2], (D,), dtype=jnp.float32)
        log_decay = jax.random.normal(ks[3], (H,), dtype=jnp.float32)
        norm_weight = jnp.ones((D,), dtype=jnp.float32)
        o_w = jax.random.normal(ks[4], (D, D), dtype=jnp.float32) * 0.02
        return {'x': x, 'q': q, 'k': k, 'log_decay': log_decay, 'norm_weight': norm_weight, 'o_w': o_w}
    _L0_attn_in = _L0_attn_setup()

    def _L0_ffn_setup():
        import jax, jax.numpy as jnp
        import numpy as np
        E = 8
        G = 4
        LG = 2
        TOPK = 2
        ROUTE_SCALE = 1.0

        def _grouped_mm(x, w, counts):
            counts = counts.astype(jnp.int32)
            if hasattr(jax.lax, 'ragged_dot'):
                return jax.lax.ragged_dot(x, w, counts)
            offs = jnp.cumsum(counts)
            eid = jnp.searchsorted(offs, jnp.arange(x.shape[0]), side='right')
            oh = jax.nn.one_hot(eid, w.shape[0], dtype=x.dtype)
            return jnp.einsum('nd,ne,edh->nh', x, oh, w)
        key = jax.random.key(seed)
        ks = jax.random.split(key, 8)
        bs, slen, dim, hid, shid = (2, 512, 256, 128, 256)
        std = 0.02
        return {'x': jax.random.normal(ks[0], (bs, slen, dim), jnp.float32), 'w_gate': jax.random.normal(ks[1], (E, dim), jnp.float32) * std, 'w1': jax.random.normal(ks[2], (E, dim, hid), jnp.float32) * std, 'w2': jax.random.normal(ks[3], (E, hid, dim), jnp.float32) * std, 'w3': jax.random.normal(ks[4], (E, dim, hid), jnp.float32) * std, 'sw1': jax.random.normal(ks[5], (shid, dim), jnp.float32) * std, 'sw2': jax.random.normal(ks[6], (dim, shid), jnp.float32) * std, 'sw3': jax.random.normal(ks[7], (shid, dim), jnp.float32) * std, 'expert_bias': jnp.zeros((E,), jnp.float32)}
    _L0_ffn_in = _L0_ffn_setup()
    _d = {'L0_attn_x': _L0_attn_in['x'], 'L0_attn_q': _L0_attn_in['q'], 'L0_attn_k': _L0_attn_in['k'], 'L0_attn_log_decay': _L0_attn_in['log_decay'], 'L0_attn_norm_weight': _L0_attn_in['norm_weight'], 'L0_attn_o_w': _L0_attn_in['o_w'], 'L0_ffn_w_gate': _L0_ffn_in['w_gate'], 'L0_ffn_w1': _L0_ffn_in['w1'], 'L0_ffn_w2': _L0_ffn_in['w2'], 'L0_ffn_w3': _L0_ffn_in['w3'], 'L0_ffn_sw1': _L0_ffn_in['sw1'], 'L0_ffn_sw2': _L0_ffn_in['sw2'], 'L0_ffn_sw3': _L0_ffn_in['sw3'], 'L0_ffn_expert_bias': _L0_ffn_in['expert_bias']}
    _x0 = _d['L0_attn_x']
    _d['L0_attn_x'] = jax.random.normal(jax.random.fold_in(jax.random.key(seed), 1), (8, 1024, 256), dtype=_x0.dtype)
    del _x0
    return _d

def reference(L0_attn_x, L0_attn_q, L0_attn_k, L0_attn_log_decay, L0_attn_norm_weight, L0_attn_o_w, L0_ffn_w_gate, L0_ffn_w1, L0_ffn_w2, L0_ffn_w3, L0_ffn_sw1, L0_ffn_sw2, L0_ffn_sw3, L0_ffn_expert_bias):

    def _L0_attn_ref(x, q, k, log_decay, norm_weight, o_w):
        import jax, jax.numpy as jnp
        import numpy as np
        H = 16
        EPS = 1e-06
        b, n, dm = x.shape
        dh = dm // H
        qh = q.reshape(H, dh)
        kh = k.reshape(H, dh)
        v = x.reshape(b, n, H, dh)
        lam = jax.nn.sigmoid(log_decay)

        def step(S, v_t):
            S = lam[None, :, None, None] * S + kh[None, :, :, None] * v_t[:, :, None, :]
            o_t = jnp.einsum('hd,bhdv->bhv', qh, S)
            return (S, o_t)
        S0 = jnp.zeros((b, H, dh, dh), dtype=x.dtype)
        _, o = jax.lax.scan(step, S0, jnp.moveaxis(v, 1, 0))
        o = jnp.moveaxis(o, 0, 1).reshape(b, n, dm)
        o = o * jax.lax.rsqrt(jnp.mean(o * o, axis=-1, keepdims=True) + EPS) * norm_weight
        return o @ o_w.T

    def _L0_ffn_ref(x, w_gate, w1, w2, w3, sw1, sw2, sw3, expert_bias):
        import jax, jax.numpy as jnp
        import numpy as np
        E = 8
        G = 4
        LG = 2
        TOPK = 2
        ROUTE_SCALE = 1.0

        def _grouped_mm(x, w, counts):
            counts = counts.astype(jnp.int32)
            if hasattr(jax.lax, 'ragged_dot'):
                return jax.lax.ragged_dot(x, w, counts)
            offs = jnp.cumsum(counts)
            eid = jnp.searchsorted(offs, jnp.arange(x.shape[0]), side='right')
            oh = jax.nn.one_hot(eid, w.shape[0], dtype=x.dtype)
            return jnp.einsum('nd,ne,edh->nh', x, oh, w)
        bs, slen, dim = x.shape
        xf = x.reshape(-1, dim)
        N = xf.shape[0]
        logits = xf @ w_gate.T
        scores = jax.nn.softmax(logits.astype(jnp.float32), axis=-1)
        original = scores
        s = (scores + expert_bias).reshape(N, G, E // G)
        group_scores = jax.lax.top_k(s, 2)[0].sum(-1)
        top_groups = jax.lax.top_k(group_scores, LG)[1]
        keep = jnp.zeros((N, G), bool).at[jnp.arange(N)[:, None], top_groups].set(True)
        masked = jnp.where(keep[:, :, None], s, -jnp.inf).reshape(N, E)
        topk_idx = jax.lax.top_k(masked, TOPK)[1]
        weights = (jnp.take_along_axis(original, topk_idx, axis=1) * ROUTE_SCALE).astype(x.dtype)
        counts = jnp.bincount(topk_idx.reshape(-1), length=E)
        flat_idx = topk_idx.reshape(-1)
        routed_in = xf[flat_idx]
        routed_in = (routed_in.astype(jnp.float32) * weights.reshape(-1, 1)).astype(x.dtype)
        h = jax.nn.silu(_grouped_mm(routed_in, w1, counts)) * _grouped_mm(routed_in, w3, counts)
        routed_out = _grouped_mm(h, w2, counts)
        shared = jax.nn.silu(xf @ sw1.T) * (xf @ sw3.T) @ sw2.T
        out = shared.at[flat_idx].add(routed_out)
        return out.reshape(bs, slen, dim)
    x = L0_attn_x
    xn = _layernorm(x, axis=-1)
    x = x + _L0_attn_ref(xn, L0_attn_q, L0_attn_k, L0_attn_log_decay, L0_attn_norm_weight, L0_attn_o_w) + _L0_ffn_ref(xn, L0_ffn_w_gate, L0_ffn_w1, L0_ffn_w2, L0_ffn_w3, L0_ffn_sw1, L0_ffn_sw2, L0_ffn_sw3, L0_ffn_expert_bias)
    return x

_drawn_inputs = setup_inputs


def setup_inputs(seed=0):
    import zlib

    import numpy as np

    out = dict(_drawn_inputs(seed))
    spreads = {'L0_attn_norm_weight': (1.0, 0.6), 'L0_ffn_expert_bias': (0.0, 0.49)}
    factors = {'L0_ffn_w_gate': 8.0,
     'L0_ffn_w1': 3.691,
     'L0_ffn_w2': 3.22,
     'L0_ffn_w3': 3.659,
     'L0_ffn_sw1': 3.57,
     'L0_ffn_sw2': 3.545,
     'L0_ffn_sw3': 3.541}
    for name, (base, spread) in spreads.items():
        noise = np.random.default_rng([zlib.crc32(name.encode()), seed]).standard_normal(out[name].shape)
        drawn = base * np.exp(spread * noise) if base else spread * noise
        out[name] = jnp.asarray(drawn.astype(out[name].dtype))
    for name, factor in factors.items():
        out[name] = (out[name] * factor).astype(out[name].dtype)
    return out
```

```python
import concourse.bass as bass
from concourse import mybir
from contextlib import ExitStack

P = 128
TOKENS, DIM = 8192, 256
KC = DIM // P
TILE = 512
TT = TILE // P
NT = TOKENS // TILE
NB = NT // 2
NTT = TOKENS // P
E = 8
GRP = 4
HID = 128
TOPK = 2
ROWT = TOPK * NTT
FIRST_ROW_TILE = NT // 2
RPT = ROWT // (NT - FIRST_ROW_TILE)
ROW_TILES = NT - FIRST_ROW_TILE
RG = 4
PAIRS = E * E
LN_EPS, RMS_EPS = 1e-5, 1e-6
FAR = 1e38
LEAST = 1.1754944e-38

C_IDENT, C_HEADS, C_THR8, C_THR4, C_POS, C_IOTA, C_PAIR = 0, 128, 256, 320, 336, 464, 472
C_END = 473
S_Q, S_K, S_NW, S_LD, S_EB, S_END = 0, 2, 4, 6, 8, 16


def build(nc, x, small, w_gate, w_up, w_down, w_o, w1, w2, w3, consts, out):
    f32, f32r, bf16 = mybir.dt.float32, mybir.dt.float32r, mybir.dt.bfloat16
    ALU = mybir.AluOpType
    ACT = mybir.ActivationFunctionType
    AX = mybir.AxisListType
    V, G, A, T = nc.vector, nc.gpsimd, nc.scalar, nc.tensor

    x_v = x.rearrange("(n p) d -> p n d", p=P)
    out_v = out.rearrange("(n p) d -> p n d", p=P)
    codes_dram = nc.dram_tensor("row_codes", (ROWT, P), bf16, kind="Internal").ap()

    ctx = ExitStack()
    with ctx:
        def sb(name, shape, dt=f32):
            return ctx.enter_context(nc.sbuf_tensor(name, shape, dt))

        def bank(name):
            return ctx.enter_context(nc.psum_tensor(name, [P, 512], f32))

        def sem(name):
            return ctx.enter_context(nc.semaphore(name))

        x_sb = sb("x_sb", [P, NTT, DIM])
        e_sb = sb("e_sb", [P, KC, TOKENS])
        raw_up = e_sb[:, 0, 1024:2048].rearrange("p (k n) -> p k n", k=KC)
        raw_down = e_sb[:, 0, 2048:2560].rearrange("p (k n) -> p k n", k=KC)
        raw_o = e_sb[:, 0, 2560:3072].rearrange("p (k n) -> p k n", k=KC)
        raw_gate = e_sb[:, 0, 3072:3072 + KC * E].rearrange("p (k n) -> p k n", k=KC)
        w1_sb = e_sb[:, 0, 4096:6144].rearrange("p (k g h) -> p k g h", k=KC, g=E)
        w3_sb = e_sb[:, 1, 4096:6144].rearrange("p (k g h) -> p k g h", k=KC, g=E)
        w2_sb = e_sb[:, 0, 0:E * DIM].rearrange("p (g d) -> p g d", g=E)
        codes_bc = e_sb[:, 1, 0:RPT * P].bitcast(bf16).rearrange("p (u n) -> p u n", u=2)

        xn = sb("xn", [P, 2, TT, DIM])
        xh = sb("xh", [P, 2, KC, TILE], f32r)
        xl = sb("xl", [P, 2, KC, TILE], f32r)
        act_out = sb("act_out", [P, 2, TILE])
        hh = sb("hh", [P, 2, 2, TILE], f32r)
        hl = sb("hl", [P, 2, 2, TILE], f32r)
        sq = sb("sq", [P, KC, TILE])
        pair_hot_t = [t[:, :, :, :].rearrange("p a b n -> p (a b n)") for t in (hh, hl)]
        pair_w = [xn[:, u, :, :].rearrange("p a (b g e) -> p (a b) g e", g=E, e=E) for u in (0, 1)]

        wup_h = sb("wup_h", [P, KC, 512], f32r)
        wup_l = sb("wup_l", [P, KC, 512], f32r)
        wdn_h = sb("wdn_h", [P, KC, DIM], f32r)
        wdn_l = sb("wdn_l", [P, KC, DIM], f32r)
        wo_h = sb("wo_h", [P, KC, DIM], f32r)
        wo_l = sb("wo_l", [P, KC, DIM], f32r)
        wg_hl = sb("wg_hl", [P, KC, 2, E], f32r)

        cst = sb("cst", [P, C_END])
        ident = cst[:, C_IDENT:C_IDENT + P]
        heads = cst[:, C_HEADS:C_HEADS + P]
        thr8 = cst[:, C_THR8:C_THR8 + 64].rearrange("p (j i) -> p j i", j=E)
        thr4 = cst[:, C_THR4:C_THR4 + 16].rearrange("p (j i) -> p j i", j=GRP)
        pos = cst[:, C_POS:C_POS + ROWT]
        iota = cst[:, C_IOTA:C_IOTA + E]
        pair_no = cst[:, C_PAIR:C_PAIR + 1]
        par = sb("par", [P, S_END])
        ones = sb("ones", [P, P])
        lam = sb("lam", [P, KC])
        qk = sb("qk", [P, KC])
        c_col = sb("c_col", [P, KC])
        o_scale = sb("o_scale", [P, KC])

        stats = sb("stats", [P, TT, 6])
        mean_var = sb("mean_var", [P, TT, 2])
        var_eps = sb("var_eps", [P, 2, TT])
        neg_mean = sb("neg_mean", [P, 2, TT])
        rstd = sb("rstd", [P, 2, TT])
        shift = sb("shift", [P, 2, TT])
        power = sb("power", [P, E])
        ms = sb("ms", [P, NTT])
        rms = sb("rms", [P, NTT])

        logit = sb("logit", [P, E, E])
        top = sb("top", [P, E])
        prob = sb("prob", [P, E, E])
        total = sb("total", [P, E])
        score = sb("score", [P, E, E])
        gscore = sb("gscore", [P, E, GRP])
        grank = sb("grank", [P, E, GRP])
        diff = sb("diff", [P, E, E, E])
        flat_diff = diff[:, :, :, :].rearrange("p t j i -> p (t j i)")
        gdiff = flat_diff[:, 0:E * GRP * GRP].rearrange("p (t j i) -> p t j i", t=E, j=GRP)
        scaled_pick = flat_diff[:, 0:2 * E * E].rearrange("p (r e) -> p r e", e=E)
        rank = sb("rank", [P, E, E])
        pick = sb("pick", [P, ROWT, E], bf16)
        pick_w = sb("pick_w", [P, ROWT, E])
        row_w = sb("row_w", [P, ROWT])
        row_e = sb("row_e", [P, ROWT])

        x8 = sb("x8", [P, KC, E])
        ab = sb("ab", [P, 3, PAIRS])
        a_hl = sb("a_hl", [P, HID], f32r)
        group_hot = sq[:, 0, :].bitcast(bf16).rearrange("p (j g) -> p j g", g=E)
        row_g = sq[:, 1, 0:ROWT]
        code = sq[:, 1, 128:128 + ROWT]
        a_t = sq[:, 1, 256:256 + HID]
        count = sb("count", [P, E])
        ends = sb("ends", [P, E])
        past = flat_diff.bitcast(bf16).rearrange("p (j g) -> p j g", g=E)
        code_t = sb("code_t", [P, P], bf16)
        row_w_now = sb("row_w_now", [P, 2, RPT])
        warm = sb("warm", [P, 1])
        s_sum = sb("s_sum", [P, PAIRS])

        tp = [bank("tp0"), bank("tp1")]
        up = [bank("up0"), bank("up1"), bank("up2")]
        dn = [bank("dn0"), bank("dn1")]
        misc = bank("misc")
        m_gate = misc[:, 0:16 * (TT - 1) + P]
        m_ssq = misc[:, 176:176 + TT - 1 + 64]
        m_ab = misc[:, 256:256 + 2 * PAIRS].rearrange("p (a c) -> p a c", a=2)
        m_wide = misc[:, 384:512]
        att = [tp, dn]

        x_in = [sem("x_in0"), sem("x_in1")]
        small_in, bias_in, cst_in = sem("small_in"), sem("bias_in"), sem("cst_in")
        up_in, wrest_in, w13_in = sem("up_in"), sem("wrest_in"), sem("w13_in")
        w2_in = sem("w2_in")
        codes_out = sem("codes_out")
        codes_in = [sem("codes_in0"), sem("codes_in1")]
        stored = sem("stored")
        setup = sem("setup")
        decay_exp, power_set, qk_sum = sem("decay_exp"), sem("power_set"), sem("qk_sum")
        params = sem("params")
        o_scaled = sem("o_scaled")
        w_hi, w_lo = sem("w_hi"), sem("w_lo")
        stat_step = sem("stat_step")
        ln_stats = sem("ln_stats")
        rstd_step, rstd_ready = sem("rstd_step"), sem("rstd_ready")
        xn_ready = sem("xn_ready")
        tp_ready = sem("tp_ready")
        xh_ready, xl_ready = sem("xh_ready"), sem("xl_ready")
        e_ready = sem("e_ready")
        up_ready = sem("up_ready")
        silu_ready, h_ready = sem("silu_ready"), sem("h_ready")
        hh_ready, hl_ready = sem("hh_ready"), sem("hl_ready")
        sq_ready, sq_added = sem("sq_ready"), sem("sq_added")
        misc_ready = sem("misc_ready")
        ms_read, logit_read = sem("ms_read"), sem("logit_read")
        dn_ready, y_ready = sem("dn_ready"), sem("y_ready")
        route = sem("route")
        exp_ready = sem("exp_ready")
        rms_ready = sem("rms_ready")
        x8_ready, ab_read = sem("x8_ready"), sem("ab_read")
        eh_ready, el_ready = sem("eh_ready"), sem("el_ready")
        att_ready = sem("att_ready")
        o_ready = sem("o_ready")
        place = sem("place")
        count_ready, code_ready, code_tr = sem("count_ready"), sem("code_ready"), sem("code_tr")
        a_tr, a_ready = sem("a_tr"), sem("a_ready")
        code_sb = sem("code_sb")
        hot_ready, pair_w_ready = sem("hot_ready"), sem("pair_w_ready")
        roww_ready = sem("roww_ready")
        gathered = sem("gathered")
        row_silu = sem("row_silu")
        reduced = sem("reduced")
        s_added = sem("s_added")
        h_pairs, routed, first8_ready = sem("h_pairs"), sem("routed"), sem("first8_ready")

        ROUTE_STEPS = 21

        def token_tile(i, t):
            return x_sb[:, bass.ds(TT * i + t, 1), :].rearrange("p a d -> p (a d)")

        block = ctx.enter_context(nc.Block())

        @block.sync
        def _(sp):
            sp.dma_start(par[:, 0:S_EB], small[:, 0:S_EB]).then_inc(small_in, 16)
            sp.dma_start(x_sb[:, 0:TT, :], x_v[:, 0:TT, :]).then_inc(x_in[0], 16)
            sp.dma_start(par[:, S_EB:S_END], small[0:1, S_EB:S_END].to_broadcast([P, E])).then_inc(bias_in, 16)
            sp.dma_start(x_sb[:, TT:2 * TT, :], x_v[:, TT:2 * TT, :]).then_inc(x_in[1], 16)
            with sp.Fori(1, NB) as b:
                for u in range(2):
                    i = 2 * b + u
                    sp.wait_ge(x_in[u], 16 * b)
                    sp.dma_start(x_sb[:, bass.ds(TT * i, TT), :],
                                 x_v[:, bass.ds(TT * i, TT), :]).then_inc(x_in[u], 16)

            sp.wait_ge(o_ready, TT)
            sp.dma_start(out_v[E:P, 0, :], x_sb[E:P, 0, :]).then_inc(stored, 16)
            sp.dma_start(out_v[:, 1:TT, :], x_sb[:, 1:TT, :]).then_inc(stored, 16)
            with sp.Fori(1, FIRST_ROW_TILE) as i:
                sp.wait_ge(o_ready, TT * i + TT)
                sp.dma_start(out_v[:, bass.ds(TT * i, TT), :],
                             x_sb[:, bass.ds(TT * i, TT), :]).then_inc(stored, 16)
            sp.wait_ge(eh_ready, FIRST_ROW_TILE)
            sp.wait_ge(el_ready, FIRST_ROW_TILE)
            sp.wait_ge(code_sb, 1)
            sp.dma_start(codes_dram, code_t[:, :]).then_inc(codes_out, 16)
            sp.wait_ge(codes_out, 16)
            for u in range(2):
                sp.dma_start(codes_bc[:, u, :], codes_dram[RPT * u:RPT * (u + 1), :]
                             .rearrange("(o j) n -> o (j n)", o=1).to_broadcast([P, RPT * P]))\
                    .then_inc(codes_in[u], 16)
            sp.dma_start(w2_sb, w2.rearrange("g h d -> h g d")).then_inc(w2_in, 16)
            with sp.Fori(0, (NT - FIRST_ROW_TILE) // 2 - 1) as b:
                for u in range(2):
                    i = FIRST_ROW_TILE + 2 * b + u
                    sp.wait_ge(hot_ready, 2 * b + u + 1)
                    sp.dma_start(codes_bc[:, u, :],
                                 codes_dram[bass.ds(RPT * (2 * b + u + 2), RPT), :]
                                 .rearrange("(o j) n -> o (j n)", o=1).to_broadcast([P, RPT * P]))\
                        .then_inc(codes_in[u], 16)
                    sp.wait_ge(o_ready, TT * i + TT)
                    sp.dma_start(out_v[:, bass.ds(TT * i, TT), :],
                                 x_sb[:, bass.ds(TT * i, TT), :]).then_inc(stored, 16)
            for i in range(NT - 2, NT):
                sp.wait_ge(o_ready, TT * i + TT)
                sp.dma_start(out_v[:, TT * i:TT * i + TT, :],
                             x_sb[:, TT * i:TT * i + TT, :]).then_inc(stored, 16)
            sp.wait_ge(first8_ready, 1)
            sp.dma_start(out[0:E, :], x_sb[0:E, 0, :]).then_inc(stored, 16)
            sp.wait_ge(stored, 16 * (NT + 2))

        @block.gpsimd
        def _(pool):
            G.memset(power[:, :], -0.5).then_inc(power_set, 1)
            pool.wait_ge(power_set, 1)

            def token_scale(i, u):
                pool.wait_ge(ln_stats, 2 * i + 2)
                if not (isinstance(i, int) and i < 2):
                    pool.wait_ge(xn_ready, TT * (i - 1))
                G.tensor_tensor(rstd[:, u, :], var_eps[:, u, :], power[:, 0:TT], ALU.pow).then_inc(rstd_step, 1)
                pool.wait_ge(rstd_step, i + 1)
                G.tensor_tensor(shift[:, u, :], neg_mean[:, u, :], rstd[:, u, :], ALU.mult).then_inc(rstd_ready, 1)

            def sum_squares(i):
                pool.wait_ge(sq_ready, 2 * i + 2)
                G.tensor_tensor(sq[:, 0, :], sq[:, 0, :], sq[:, 1, :], ALU.add).then_inc(sq_added, 1)

            def h_lo(i, u, m):
                pool.wait_ge(hh_ready, 2 * i + m + 1)
                G.tensor_tensor(hl[:, u, m, :], act_out[:, m, :], hh[:, u, m, :].bitcast(f32),
                                ALU.subtract).then_inc(hl_ready, 1)

            def rms_factors(b):
                pool.wait_ge(ms_read, 2 * b + 2)
                at = bass.ds(E * b, E)
                G.tensor_tensor(rms[:, at], ms[:, at], power[:, :], ALU.pow).then_inc(rms_ready, 1)

            def batch(b, first=False, last=False):
                for u in range(2):
                    i = 2 * b + u
                    if not (first and u == 0):
                        sum_squares(i - 1)
                    h_lo(i, u, 0)
                    if u == 1 and not first:
                        rms_factors(b - 1)
                    if not last:
                        token_scale(i + 2, u)
                    h_lo(i, u, 1)

            def weight_lo(lo, hi, raw, n):
                pool.wait_ge(w_hi, n)
                G.tensor_tensor(lo, raw, hi.bitcast(f32), ALU.subtract).then_inc(w_lo, 1)

            token_scale(0, 0)
            weight_lo(wup_l[:, :, :], wup_h[:, :, :], raw_up, 1)
            weight_lo(wg_hl[:, :, 1, :], wg_hl[:, :, 0, :], raw_gate, 2)
            token_scale(1, 1)
            weight_lo(wdn_l[:, :, :], wdn_h[:, :, :], raw_down, 3)
            weight_lo(wo_l[:, :, :], wo_h[:, :, :], raw_o, 4)
            batch(0, first=True)
            with pool.Fori(1, NB - 1) as b:
                batch(b)
            batch(NB - 1, last=True)
            sum_squares(NT - 1)

            def e_lo(i, u):
                pool.wait_ge(eh_ready, i + 1)
                G.tensor_tensor(xl[:, u, :, :], e_sb[:, :, bass.ds(TILE * i, TILE)], xh[:, u, :, :].bitcast(f32),
                                ALU.subtract).then_inc(el_ready, 1)

            e_lo(0, 0)
            e_lo(1, 1)
            rms_factors(NB - 1)
            with pool.Fori(1, NB) as b:
                for u in range(2):
                    e_lo(2 * b + u, u)

        @block.scalar
        def _(act):
            act.dma_start(raw_up, w_up.rearrange("(k p) n -> p k n", p=P)).then_inc(up_in, 16)
            act.dma_start(raw_gate, w_gate.rearrange("(k p) n -> p k n", p=P)).then_inc(up_in, 16)
            act.dma_start(cst[:, :], consts).then_inc(cst_in, 16)
            act.dma_start(raw_down, w_down.rearrange("(k p) n -> p k n", p=P)).then_inc(wrest_in, 16)
            act.dma_start(raw_o, w_o.rearrange("(k p) n -> p k n", p=P)).then_inc(wrest_in, 16)
            for k in range(KC):
                act.dma_start(w1_sb[:, k, :, :], w1[:, k * P:(k + 1) * P, :].rearrange("g p h -> p g h"))\
                    .then_inc(w13_in, 16)
                act.dma_start(w3_sb[:, k, :, :], w3[:, k * P:(k + 1) * P, :].rearrange("g p h -> p g h"))\
                    .then_inc(w13_in, 16)
            act.wait_ge(small_in, 16)
            A.activation(lam[:, :], par[:, S_LD:S_LD + KC], ACT.Exp, scale=-1.0).then_inc(decay_exp, 1)

            def normalize(i, u):
                act.wait_ge(rstd_ready, i + 1)
                if not (isinstance(i, int) and i < 2):
                    act.wait_ge(tp_ready, 2 * i - 2)
                for t in range(TT):
                    A.activation(xn[:, u, t, :], token_tile(i, t), ACT.Identity, bias=shift[:, u, t:t + 1],
                                 scale=rstd[:, u, t:t + 1]).then_inc(xn_ready, 1)

            def x_hi(i, u):
                for k in range(KC):
                    act.wait_ge(tp_ready, 2 * i + k + 1)
                    A.activation(xh[:, u, k, :], tp[k][:, :], ACT.Copy).then_inc(xh_ready, 1)

            def silu(i, m, first=False):
                act.wait_ge(up_ready, 4 * i + 2 * m + 1)
                if not first:
                    act.wait_ge(hl_ready, 2 * i + m - 1)
                A.activation(act_out[:, m, :], up[2 * m][:, :], ACT.Silu).then_inc(silu_ready, 1)

            def h_hi(i, u, m, first=False):
                act.wait_ge(h_ready, 2 * i + m + 1)
                if not first:
                    act.wait_ge(dn_ready, 2 * i - 2)
                A.activation(hh[:, u, m, :], act_out[:, m, :], ACT.Copy).then_inc(hh_ready, 1)

            def squares(i, first=False):
                act.wait_ge(e_ready, 2 * i + 2)
                if not first:
                    act.wait_ge(misc_ready, i + 1)
                for k in range(KC):
                    A.activation(sq[:, k, :], e_sb[:, k, bass.ds(TILE * i, TILE)], ACT.Square,
                                 scale=c_col[:, k:k + 1]).then_inc(sq_ready, 1)

            def router_exp(b):
                act.wait_ge(route, ROUTE_STEPS * b + 2)
                A.activation(prob[:, :, :], prob[:, :, :], ACT.Exp).then_inc(exp_ready, 1)

            def batch(b, first=False, last=False):
                for u in range(2):
                    i = 2 * b + u
                    silu(i, 0, first and u == 0)
                    if not (first and u == 0):
                        squares(i - 1, first)
                    if not (last and u == 1):
                        x_hi(i + 1, 1 - u)
                    h_hi(i, u, 0, first)
                    silu(i, 1, first and u == 0)
                    h_hi(i, u, 1, first)
                    if not last:
                        normalize(i + 2, u)
                    if u == 0 and not first:
                        router_exp(b - 1)

            def weight_hi(hi, raw):
                A.activation(hi, raw, ACT.Copy).then_inc(w_hi, 1)

            act.wait_ge(up_in, 32)
            weight_hi(wup_h[:, :, :], raw_up)
            normalize(0, 0)
            weight_hi(wg_hl[:, :, 0, :], raw_gate)
            x_hi(0, 0)
            normalize(1, 1)
            act.wait_ge(wrest_in, 32)
            weight_hi(wdn_h[:, :, :], raw_down)
            act.wait_ge(params, 1)
            for k in range(KC):
                A.activation(raw_o[:, k, :], raw_o[:, k, :], ACT.Copy, scale=o_scale[:, k:k + 1])\
                    .then_inc(o_scaled, 1)
            act.wait_ge(o_scaled, KC)
            weight_hi(wo_h[:, :, :], raw_o)
            batch(0, first=True)
            with act.Fori(1, NB - 1) as b:
                batch(b)
            batch(NB - 1, last=True)
            squares(NT - 1)

            def e_hi(i, u, first=False):
                if first:
                    act.wait_ge(misc_ready, NT)
                else:
                    act.wait_ge(att_ready, 2 * i - 2)
                A.activation(xh[:, u, :, :], e_sb[:, :, bass.ds(TILE * i, TILE)], ACT.Copy).then_inc(eh_ready, 1)

            e_hi(0, 0, first=True)
            e_hi(1, 1, first=True)
            router_exp(NB - 1)
            with act.Fori(1, FIRST_ROW_TILE // 2) as b:
                for u in range(2):
                    e_hi(2 * b + u, u)

            e_hi(FIRST_ROW_TILE, 0)
            A.activation(warm[:, :], ones[:, 0:1], ACT.Silu)

            def rows(n, u, last=False):
                    if not last:
                        e_hi(FIRST_ROW_TILE + n + 1, 1 - u)
                    act.wait_ge(roww_ready, n + 1)
                    for q in range(RPT // RG):
                        act.wait_ge(gathered, (RPT // RG) * n + q + 1)
                        if q >= 2:
                            act.wait_ge(reduced, (RPT // RG) * n + q - 1)
                        for r in range(RG):
                            j = RG * q + r
                            A.activation(act_out[:, q % 2, r * HID:(r + 1) * HID],
                                         up[q % 2][:, r * HID:(r + 1) * HID], ACT.Silu,
                                         scale=row_w_now[:, u, j:j + 1]).then_inc(row_silu, 1)

            with act.Fori(0, ROW_TILES // 2 - 1) as b:
                rows(2 * b, 0)
                rows(2 * b + 1, 1)
            rows(ROW_TILES - 2, 0)
            rows(ROW_TILES - 1, 1, last=True)

        @block.vector
        def _(dve):
            at_setup = 0

            def done(ins):
                nonlocal at_setup
                at_setup += 1
                ins.then_inc(setup, 1)
                dve.wait_ge(setup, at_setup)

            def bn(i):
                for t in range(TT):
                    V.bn_stats(stats[:, t, :], token_tile(i, t)).then_inc(stat_step, 1)

            def wait_bn(i):
                dve.wait_ge(stat_step, 2 * TT * i + TT)

            def aggregate(i):
                for t in range(TT):
                    V.bn_aggr(mean_var[:, t, :], stats[:, t, :]).then_inc(stat_step, 1)

            def finish_stats(i, u):
                dve.wait_ge(stat_step, 2 * TT * i + 2 * TT)
                if not (isinstance(i, int) and i < 2):
                    dve.wait_ge(rstd_ready, i - 1)
                V.tensor_scalar(var_eps[:, u, :], mean_var[:, :, 1], LN_EPS, None, ALU.add).then_inc(ln_stats, 1)
                V.tensor_scalar(neg_mean[:, u, :], mean_var[:, :, 0], -1.0, None, ALU.mult).then_inc(ln_stats, 1)

            def x_lo(i, u, k):
                dve.wait_ge(xh_ready, 2 * i + k + 1)
                V.tensor_tensor(xl[:, u, k, :], tp[k][:, :], xh[:, u, k, :].bitcast(f32),
                                ALU.subtract).then_inc(xl_ready, 1)

            def scan(i, u, k):
                if u:
                    dve.wait_ge(e_ready, 2 * i + k - 1)
                start = e_sb[:, k, bass.ds(TILE * i - 1, 1)] if u else 0.0
                V.tensor_tensor_scan(e_sb[:, k, bass.ds(TILE * i, TILE)], lam[:, k:k + 1].to_broadcast([P, TILE]),
                                     tp[k][:, :], start, ALU.mult, ALU.add).then_inc(e_ready, 1)

            def gate_mul(i, m):
                dve.wait_ge(silu_ready, 2 * i + m + 1)
                dve.wait_ge(up_ready, 4 * i + 2 * m + 2)
                V.tensor_tensor(act_out[:, m, :], act_out[:, m, :], up[1 - m][:, :], ALU.mult).then_inc(h_ready, 1)

            def add_shared(i, a):
                dve.wait_ge(dn_ready, 2 * i + a + 1)
                at = x_sb[:, bass.ds(TT * i + 2 * a, 2), :]
                V.tensor_tensor(at, dn[a][:, :].rearrange("p (t d) -> p t d", t=2), at, ALU.add).then_inc(y_ready, 1)

            def read_mean_square(i):
                dve.wait_ge(misc_ready, i + 2)
                V.tensor_scalar(ms[:, bass.ds(TT * i, TT)], m_ssq[:, 0:TT], 1.0 / DIM, RMS_EPS, ALU.mult, ALU.add)\
                    .then_inc(ms_read, 1)

            def read_logits(i, u):
                dve.wait_ge(misc_ready, i + 1)
                V.tensor_reduce(logit[:, TT * u:TT * u + TT, :],
                                m_gate[:, 0:16 * TT].rearrange("p (t h e) -> p t e h", h=2, e=E), AX.X,
                                ALU.add).then_inc(logit_read, 1)

            def after(b, n):
                dve.wait_ge(route, ROUTE_STEPS * b + n)

            def over_experts(t):
                return t[:, :].unsqueeze(2).to_broadcast([P, E, E])

            def route_max(b):
                dve.wait_ge(logit_read, 2 * b + 2)
                V.tensor_reduce(top[:, :], logit[:, :, :], AX.X, ALU.max).then_inc(route, 1)

            def route_shift(b):
                after(b, 1)
                V.tensor_tensor(prob[:, :, :], logit[:, :, :], over_experts(top), ALU.subtract).then_inc(route, 1)

            def route_total(b):
                dve.wait_ge(exp_ready, b + 1)
                V.tensor_reduce(total[:, :], prob[:, :, :], AX.X, ALU.add).then_inc(route, 1)

            def route_invert(b):
                after(b, 3)
                V.reciprocal(total[:, :], total[:, :]).then_inc(route, 1)

            def route_prob(b):
                after(b, 4)
                V.tensor_tensor(prob[:, :, :], prob[:, :, :], over_experts(total), ALU.mult).then_inc(route, 1)

            def route_score(b):
                after(b, 5)
                V.tensor_tensor(score[:, :, :], prob[:, :, :],
                                par[:, S_EB:S_END].unsqueeze(1).to_broadcast([P, E, E]), ALU.add).then_inc(route, 1)

            score_pairs = score[:, :, :].rearrange("p t (g h) -> p t g h", h=2)

            def route_group_score(b):
                after(b, 6)
                V.tensor_tensor(gscore[:, :, :], score_pairs[:, :, :, 0], score_pairs[:, :, :, 1],
                                ALU.add).then_inc(route, 1)

            def route_group_diff(b):
                after(b, 7)
                V.tensor_tensor(gdiff, gscore[:, :, :].unsqueeze(2).to_broadcast([P, E, GRP, GRP]),
                                gscore[:, :, :].unsqueeze(3).to_broadcast([P, E, GRP, GRP]),
                                ALU.subtract).then_inc(route, 1)

            def route_group_before(b):
                after(b, 8)
                V.tensor_tensor(gdiff, gdiff, thr4.unsqueeze(1).to_broadcast([P, E, GRP, GRP]),
                                ALU.is_ge).then_inc(route, 1)

            def route_group_rank(b):
                after(b, 9)
                V.tensor_reduce(grank[:, :, :], gdiff, AX.X, ALU.add).then_inc(route, 1)

            def route_group_penalty(b):
                after(b, 10)
                V.tensor_scalar(grank[:, :, :], grank[:, :, :], 1.5, -FAR, ALU.is_gt, ALU.mult).then_inc(route, 1)

            def route_mask(b):
                after(b, 11)
                V.tensor_tensor(score_pairs, score_pairs,
                                grank[:, :, :].unsqueeze(3).to_broadcast([P, E, GRP, 2]), ALU.add).then_inc(route, 1)

            def route_diff(b):
                after(b, 12)
                V.tensor_tensor(diff[:, :, :, :], score[:, :, :].unsqueeze(2).to_broadcast([P, E, E, E]),
                                score[:, :, :].unsqueeze(3).to_broadcast([P, E, E, E]), ALU.subtract).then_inc(route, 1)

            def route_before(b):
                after(b, 13)
                V.tensor_tensor(diff[:, :, :, :], diff[:, :, :, :],
                                thr8.unsqueeze(1).to_broadcast([P, E, E, E]), ALU.is_ge).then_inc(route, 1)

            def route_rank(b):
                after(b, 14)
                V.tensor_reduce(rank[:, :, :], diff[:, :, :, :], AX.X, ALU.add).then_inc(route, 1)

            def rows_of(b):
                return bass.ds(2 * E * b, 2 * E)

            def choices(t, b):
                return t[:, rows_of(b), :].rearrange("p (t k) e -> p t k e", k=TOPK)

            def route_pick(b):
                after(b, 15)
                for k in range(TOPK):
                    V.tensor_scalar(choices(pick, b)[:, :, k, :], rank[:, :, :], float(k), None,
                                    ALU.is_equal).then_inc(route, 1)

            def route_pick_weight(b):
                after(b, 17)
                V.tensor_tensor(choices(pick_w, b), choices(pick, b),
                                prob[:, :, :].unsqueeze(2).to_broadcast([P, E, TOPK, E]), ALU.mult).then_inc(route, 1)

            def route_pick_number(b):
                after(b, 17)
                V.tensor_tensor(scaled_pick, pick[:, rows_of(b), :],
                                iota.unsqueeze(1).to_broadcast([P, 2 * E, E]), ALU.mult).then_inc(route, 1)

            def route_row_weight(b):
                after(b, 18)
                V.tensor_reduce(row_w[:, rows_of(b)], pick_w[:, rows_of(b), :], AX.X, ALU.add).then_inc(route, 1)

            def route_row_expert(b):
                after(b, 19)
                V.tensor_reduce(row_e[:, rows_of(b)], scaled_pick, AX.X, ALU.add).then_inc(route, 1)

            V.memset(ones[:, :], 1.0)
            V.memset(s_sum[:, :], 0.0).then_inc(s_added, 1)
            dve.wait_ge(small_in, 16)
            done(V.tensor_tensor(qk[:, :], par[:, S_Q:S_Q + KC], par[:, S_K:S_K + KC], ALU.mult))
            dve.wait_ge(x_in[0], 16)
            bn(0)
            wait_bn(0)
            aggregate(0)
            finish_stats(0, 0)
            dve.wait_ge(decay_exp, 1)
            done(V.tensor_scalar(lam[:, :], lam[:, :], 1.0, None, ALU.add))
            done(V.reciprocal(lam[:, :], lam[:, :]))
            dve.wait_ge(qk_sum, 1)
            done(V.tensor_copy(c_col[:, :], m_wide[:, 0:KC]))
            V.tensor_tensor(o_scale[:, :], c_col[:, :], par[:, S_NW:S_NW + KC], ALU.mult).then_inc(params, 1)
            for k in range(KC):
                x_lo(0, 0, k)
            for k in range(KC):
                V.tensor_copy(x8[:, k, :], tp[k][:, 0:E]).then_inc(x8_ready, 1)
            for k in range(KC):
                scan(0, 0, k)
            dve.wait_ge(x_in[1], 16)
            bn(1)
            wait_bn(1)
            aggregate(1)
            finish_stats(1, 1)
            dve.wait_ge(bias_in, 16)

            def read_tables():
                dve.wait_ge(misc_ready, 1)
                for a in range(2):
                    V.tensor_copy(ab[:, a, :], m_ab[:, 0, :]).then_inc(ab_read, 1)
                V.tensor_copy(ab[:, 2, :], m_ab[:, 1, :]).then_inc(ab_read, 1)

            def batch(b, first=False, last=False):
                r = b - 1
                i = 2 * b
                if not first:
                    read_mean_square(i - 2)
                    read_logits(i - 1, 1)
                    add_shared(i - 2, 0)
                    route_max(r)
                    add_shared(i - 2, 1)
                    route_shift(r)
                if not last:
                    dve.wait_ge(x_in[0], 16 * (b + 2))
                    bn(i + 2)
                    wait_bn(i + 2)
                gate_mul(i, 0)
                if not last:
                    aggregate(i + 2)
                x_lo(i + 1, 1, 0)
                x_lo(i + 1, 1, 1)
                if not last:
                    finish_stats(i + 2, 0)
                scan(i + 1, 1, 0)
                scan(i + 1, 1, 1)
                gate_mul(i, 1)

                if first:
                    read_tables()

                i = 2 * b + 1
                if not first:
                    read_mean_square(i - 2)
                read_logits(i - 1, 0)
                if not first:
                    add_shared(i - 2, 0)
                    route_total(r)
                    add_shared(i - 2, 1)
                    route_invert(r)
                    route_prob(r)
                if not last:
                    dve.wait_ge(x_in[1], 16 * (b + 2))
                    bn(i + 2)
                    wait_bn(i + 2)
                if not first:
                    route_score(r)
                gate_mul(i, 0)
                if not last:
                    aggregate(i + 2)
                if not first:
                    route_group_score(r)
                if not last:
                    x_lo(i + 1, 0, 0)
                if not first:
                    route_group_diff(r)
                if not last:
                    x_lo(i + 1, 0, 1)
                if not first:
                    route_group_before(r)
                if not last:
                    finish_stats(i + 2, 1)
                    scan(i + 1, 0, 0)
                if not first:
                    route_group_rank(r)
                if not last:
                    scan(i + 1, 0, 1)
                if not first:
                    route_group_penalty(r)
                gate_mul(i, 1)
                if not first:
                    route_mask(r)
                    route_diff(r)
                    route_before(r)
                    route_rank(r)
                    route_pick(r)
                    route_pick_weight(r)
                    route_pick_number(r)
                    route_row_weight(r)
                    route_row_expert(r)

            batch(0, first=True)
            with dve.Fori(1, NB - 1) as b:
                batch(b)
            batch(NB - 1, last=True)
            read_mean_square(NT - 2)
            read_logits(NT - 1, 1)
            route_max(NB - 1)
            add_shared(NT - 2, 0)
            route_shift(NB - 1)
            add_shared(NT - 2, 1)

            def add_attention(i, u, tiles=range(TT)):
                for t in tiles:
                    if t % 2 == 0:
                        dve.wait_ge(att_ready, 2 * i + t // 2 + 1)
                    at = token_tile(i, t)
                    V.scalar_tensor_tensor(at, att[u][t // 2][:, (t % 2) * DIM:(t % 2 + 1) * DIM],
                                           rms[:, bass.ds(TT * i + t, 1)], at, ALU.mult, ALU.add).then_inc(o_ready, 1)

            last = NB - 1
            route_total(last)
            route_invert(last)
            add_shared(NT - 1, 0)
            route_prob(last)
            add_shared(NT - 1, 1)
            route_score(last)
            read_mean_square(NT - 1)
            route_group_score(last)
            dve.wait_ge(rms_ready, NB)
            dve.wait_ge(y_ready, 2 * NT)
            add_attention(0, 0, (0,))
            route_group_diff(last)
            add_attention(0, 0, (1,))
            route_group_before(last)
            add_attention(0, 0, (2,))
            route_group_rank(last)
            add_attention(0, 0, (3,))
            route_group_penalty(last)
            add_attention(1, 1, (0,))
            route_mask(last)
            add_attention(1, 1, (1,))
            route_diff(last)
            add_attention(1, 1, (2,))
            route_before(last)
            add_attention(1, 1, (3,))
            route_rank(last)
            add_attention(2, 0, (0,))
            route_pick(last)
            add_attention(2, 0, (1,))
            dve.wait_ge(route, ROUTE_STEPS * NB - 4)
            V.tensor_reduce(count[:, :], pick[:, :, :].rearrange("p j e -> p e j"), AX.X, ALU.add).then_inc(place, 1)
            route_pick_weight(last)
            route_pick_number(last)
            add_attention(2, 0, (2,))
            route_row_weight(last)
            route_row_expert(last)
            add_attention(2, 0, (3,))
            dve.wait_ge(count_ready, 1)
            V.tensor_tensor_scan(ends[:, :], ones[:, 0:E], m_wide[:, 0:E], 0.0, ALU.mult, ALU.add).then_inc(place, 1)
            add_attention(3, 1, (0,))
            dve.wait_ge(place, 2)
            V.tensor_tensor(past, pos.unsqueeze(2).to_broadcast([P, ROWT, E]),
                            ends[:, :].unsqueeze(1).to_broadcast([P, ROWT, E]), ALU.is_ge).then_inc(place, 1)
            add_attention(3, 1, (1,))
            dve.wait_ge(place, 3)
            V.tensor_reduce(row_g, past, AX.X, ALU.add).then_inc(place, 1)
            add_attention(3, 1, (2,))
            dve.wait_ge(place, 4)
            V.scalar_tensor_tensor(code, row_g, float(E), row_e[:, :], ALU.mult, ALU.add)\
                .then_inc(code_ready, 1)
            add_attention(3, 1, (3,))
            add_attention(4, 0, (0, 1))
            dve.wait_ge(code_tr, 1)
            V.tensor_copy(code_t[:, :], m_wide).then_inc(code_sb, 1)
            V.tensor_tensor(group_hot, row_g.unsqueeze(2).to_broadcast([P, ROWT, E]),
                            iota.unsqueeze(1).to_broadcast([P, ROWT, E]), ALU.is_equal).then_inc(place, 1)
            add_attention(4, 0, (2, 3))
            dve.wait_ge(a_tr, 1)
            V.tensor_copy(a_t, m_wide).then_inc(place, 1)
            V.tensor_copy(a_hl[:, :], m_wide).then_inc(place, 1)
            add_attention(5, 1, (0, 1))
            dve.wait_ge(place, 7)
            V.tensor_tensor(a_hl[PAIRS:P, :], a_t[PAIRS:P, :], a_hl[PAIRS:P, :].bitcast(f32), ALU.subtract)\
                .then_inc(a_ready, 1)
            add_attention(5, 1, (2, 3))
            add_attention(6, 0)
            add_attention(7, 1)

            def row_operands(n, u, turn):
                rows = bass.ds(RPT * n, RPT)
                dve.wait_ge(codes_in[u], 16 * turn + 16)
                V.tensor_scalar(pair_hot_t[u].bitcast(f32r), codes_bc[:, u, :], pair_no, None,
                                ALU.is_equal).then_inc(hot_ready, 1)
                V.tensor_copy(row_w_now[:, u, :], row_w[:, rows]).then_inc(roww_ready, 1)
                V.tensor_tensor(pair_w[u], group_hot[:, rows, :].unsqueeze(3).to_broadcast([P, RPT, E, E]),
                                pick_w[:, rows, :].unsqueeze(2).to_broadcast([P, RPT, E, E]),
                                ALU.mult).then_inc(pair_w_ready, 1)

            def add_pair_sums(n):
                dve.wait_ge(reduced, (RPT // RG) * (n + 1))
                dve.wait_ge(s_added, n + 1)
                V.tensor_tensor(s_sum[:, :], s_sum[:, :], up[2][:, 0:PAIRS], ALU.add).then_inc(s_added, 1)

            row_operands(0, 0, 0)
            with dve.Fori(0, ROW_TILES // 2 - 1) as b:
                row_operands(2 * b + 1, 1, b)
                add_attention(FIRST_ROW_TILE + 2 * b, 0)
                add_pair_sums(2 * b)
                row_operands(2 * b + 2, 0, b + 1)
                add_attention(FIRST_ROW_TILE + 2 * b + 1, 1)
                add_pair_sums(2 * b + 1)
            row_operands(ROW_TILES - 1, 1, ROW_TILES // 2 - 1)
            add_attention(NT - 2, 0)
            add_pair_sums(ROW_TILES - 2)
            add_attention(NT - 1, 1)
            add_pair_sums(ROW_TILES - 1)
            dve.wait_ge(s_added, NT - FIRST_ROW_TILE + 1)
            V.tensor_tensor(s_sum[:, :], s_sum[:, :], ab[:, 2, :], ALU.mult).then_inc(h_pairs, 1)
            dve.wait_ge(routed, 1)
            V.tensor_tensor(x_sb[0:E, 0, :], x_sb[0:E, 0, :], misc[0:E, 0:DIM], ALU.add).then_inc(first8_ready, 1)

        @block.tensor
        def _(pe):
            def parts(w_h, w_l, a_h, a_l):
                return [(w_h, a_h), (w_l, a_h), (w_h, a_l)]

            def transposes(i, u, first=False):
                pe.wait_ge(xn_ready, TT * i + TT)
                if not first:
                    pe.wait_ge(e_ready, 2 * i)
                for k in range(KC):
                    for t in range(TT):
                        last = T.transpose(tp[k][:, t * P:(t + 1) * P], xn[:, u, t, k * P:(k + 1) * P], ident)
                    last.then_inc(tp_ready, 1)

            def up_half(i, u, m, first=False):
                for n in range(2):
                    if m == 0 and n == 0:
                        if not first:
                            pe.wait_ge(h_ready, 2 * i)
                    if m == 1 and n == 1:
                        pe.wait_ge(silu_ready, 2 * i + 1)
                    to = up[(2 * m + n) % 3]
                    cols = slice(n * DIM + m * P, n * DIM + (m + 1) * P)
                    run = [(w[:, k, cols], a[:, u, k, :]) for w, a in parts(wup_h, wup_l, xh, xl) for k in range(KC)]
                    for j, (w, a) in enumerate(run):
                        last = T.matmul(to[:, :], w, a, start=(j == 0), stop=(j == len(run) - 1))
                    last.then_inc(up_ready, 1)

            def gate(u, t):
                tok = slice(t * P, (t + 1) * P)
                run = [(a[:, u, k, tok],
                        wg_hl[:, k, :, :].rearrange("p h e -> p (h e)").unsqueeze(1).to_broadcast([P, 8, 16]))
                       for a in (xh, xl) for k in range(KC)]
                for j, (a, w) in enumerate(run):
                    last = T.matmul(m_gate[:, 16 * t:16 * t + P].rearrange("p (r n) -> p r n", r=8), a, w,
                                    start=(j == 0), stop=(j == len(run) - 1))
                return last

            def square_sum(t):
                return T.matmul(m_ssq[:, t:t + 64], sq[:, 0, t * P:(t + 1) * P], ones[:, 0:64], start=True, stop=True)

            def wait_down(i, first=False):
                if first:
                    pe.wait_ge(w_lo, 3)
                pe.wait_ge(hl_ready, 2 * i + 2)
                if not first:
                    pe.wait_ge(y_ready, 2 * i)

            def down(u, t):
                tok = slice(t * P, (t + 1) * P)
                run = [(a[:, u, k, tok], w[:, k, :]) for w, a in parts(wdn_h, wdn_l, hh, hl) for k in range(KC)]
                for j, (a, w) in enumerate(run):
                    last = T.matmul(dn[t // 2][:, (t % 2) * DIM:(t % 2 + 1) * DIM], a, w,
                                    start=(j == 0), stop=(j == len(run) - 1))
                if t % 2:
                    last.then_inc(dn_ready, 1)

            def tables():
                pe.wait_ge(w13_in, 64)
                pe.wait_ge(x8_ready, 2)
                for a, w in enumerate((w1_sb, w3_sb)):
                    for g in range(E):
                        for k in range(KC):
                            T.matmul(m_ab[:, a, E * g:E * g + E], w[:, k, g, :], x8[:, k, :],
                                            start=(k == 0), stop=(k == KC - 1))

            def batch(b, first=False, last=False):
                for u in range(2):
                    i = 2 * b + u
                    up_half(i, u, 0, first and u == 0)
                    if not (last and u == 1):
                        transposes(i + 1, 1 - u)
                    up_half(i, u, 1)
                    if first and u == 0:
                        tables()
                        for t in range(TT):
                            done = gate(u, t)
                    else:
                        wait_down(i - 1, first)
                        for t in range(TT):
                            down(1 - u, t)
                        pe.wait_ge(logit_read, i)
                        if first:
                            pe.wait_ge(ab_read, 3)
                        for t in range(TT):
                            gate(u, t)
                        pe.wait_ge(sq_added, i)
                        for t in range(TT):
                            done = square_sum(t)
                    done.then_inc(misc_ready, 1)

            pe.wait_ge(cst_in, 16)
            pe.wait_ge(setup, 1)
            T.matmul(m_wide[:, 0:KC], heads, qk[:, :], start=True, stop=True).then_inc(qk_sum, 1)
            transposes(0, 0, first=True)
            pe.wait_ge(w_lo, 2)
            pe.wait_ge(xl_ready, 2)
            batch(0, first=True)
            with pe.Fori(1, NB - 1) as b:
                batch(b)
            batch(NB - 1, last=True)

            def attention(i, u, tiles=range(TT)):
                if tiles[0] == 0:
                    pe.wait_ge(el_ready, i + 1)
                for t in tiles:
                    tok = slice(t * P, (t + 1) * P)
                    run = [(a[:, u, k, tok], w[:, k, :]) for w, a in parts(wo_h, wo_l, xh, xl) for k in range(KC)]
                    for j, (a, w) in enumerate(run):
                        last = T.matmul(att[u][t // 2][:, (t % 2) * DIM:(t % 2 + 1) * DIM], a, w,
                                        start=(j == 0), stop=(j == len(run) - 1))
                    if t % 2:
                        last.then_inc(att_ready, 1)

            pe.wait_ge(w_lo, 4)
            attention(0, 0)
            wait_down(NT - 1)
            for t in range(TT):
                down(1, t)
            pe.wait_ge(logit_read, NT)
            pe.wait_ge(sq_added, NT)
            for t in range(TT):
                done = square_sum(t)
            done.then_inc(misc_ready, 1)
            pe.wait_ge(y_ready, 2 * NT)
            attention(1, 1)
            pe.wait_ge(o_ready, TT)
            attention(2, 0)
            pe.wait_ge(ms_read, NT)
            pe.wait_ge(place, 1)
            T.matmul(m_wide[:, 0:E], ones[:, :], count[:, :], start=True, stop=True).then_inc(count_ready, 1)
            pe.wait_ge(o_ready, 2 * TT)
            attention(3, 1)
            pe.wait_ge(o_ready, 3 * TT)
            attention(4, 0)
            pe.wait_ge(code_ready, 1)
            T.transpose(m_wide, code, ident).then_inc(code_tr, 1)
            pe.wait_ge(o_ready, 4 * TT)
            attention(5, 1)
            pe.wait_ge(code_sb, 1)
            T.transpose(m_wide, ab[:, 0:2, :].rearrange("p a c -> p (a c)"), ident).then_inc(a_tr, 1)
            for i in range(6, FIRST_ROW_TILE):
                pe.wait_ge(o_ready, TT * (i - 1))
                attention(i, i % 2)

            def gather(n, u, q):
                for r in range(RG):
                    j = RG * q + r
                    last = T.matmul(up[q % 2][:, r * HID:(r + 1) * HID],
                                    pair_hot_t[u][:, j * P:(j + 1) * P], a_hl[:, :], start=True, stop=True)
                last.then_inc(gathered, 1)

            def reduce(n, u, q):
                pe.wait_ge(row_silu, RPT * n + RG * (q + 1))
                for r in range(RG):
                    j = RG * q + r
                    last = T.matmul(up[2][:, 0:PAIRS], act_out[:, q % 2, r * HID:(r + 1) * HID],
                                    pair_w[u][:, j, :, :].rearrange("p g e -> p (g e)"),
                                    start=(j == 0), stop=(j == RPT - 1))
                last.then_inc(reduced, 1)

            pe.wait_ge(a_ready, 1)
            with pe.Fori(0, ROW_TILES // 2) as b:
                for u in range(2):
                    n = 2 * b + u
                    i = FIRST_ROW_TILE + n
                    pe.wait_ge(hot_ready, n + 1)
                    gather(n, u, 0)
                    gather(n, u, 1)
                    pe.wait_ge(o_ready, TT * (i - 1))
                    attention(i, u, (0,))
                    pe.wait_ge(pair_w_ready, n + 1)
                    pe.wait_ge(s_added, n + 1)
                    for q in range(RPT // RG):
                        reduce(n, u, q)
                        if q + 2 < RPT // RG:
                            gather(n, u, q + 2)
                        if q + 1 < TT:
                            attention(i, u, (q + 1,))
            pe.wait_ge(w2_in, 16)
            pe.wait_ge(h_pairs, 1)
            for g in range(E):
                last = T.matmul(misc[0:E, 0:DIM], s_sum[:, E * g:E * g + E], w2_sb[:, g, :],
                                start=(g == 0), stop=(g == E - 1))
            last.then_inc(routed, 1)


def constants():
    import numpy as np

    c = np.zeros((P, C_END), np.float32)
    p = np.arange(P)
    c[:, C_IDENT:C_IDENT + P] = np.eye(P)
    c[:, C_HEADS:C_HEADS + P] = (p[:, None] // 16 == p[None, :] // 16)
    for col, n in ((C_THR8, E), (C_THR4, GRP)):
        j, i = np.divmod(np.arange(n * n), n)
        c[:, col:col + n * n] = np.where(i < j, 0.0, LEAST)[None, :]
    j = np.arange(ROWT)
    c[:, C_POS:C_POS + ROWT] = 2 * P * (j // 2)[None, :] + 2 * p[:, None] + (j % 2)[None, :]
    c[:, C_IOTA:C_IOTA + E] = np.arange(E)
    c[:, C_PAIR] = p % PAIRS
    return c


def kernel(L0_attn_x, L0_attn_q, L0_attn_k, L0_attn_log_decay, L0_attn_norm_weight, L0_attn_o_w,
           L0_ffn_w_gate, L0_ffn_w1, L0_ffn_w2, L0_ffn_w3, L0_ffn_sw1, L0_ffn_sw2, L0_ffn_sw3,
           L0_ffn_expert_bias):
    import numpy as np
    import concourse.bacc as bacc
    from concourse.bass_utils import run_bass_kernel_spmd

    x = np.asarray(L0_attn_x)
    small = np.zeros((P, S_END), np.float32)

    def columns(v):
        return np.asarray(v).reshape(KC, P).T

    small[:, S_Q:S_Q + KC] = columns(L0_attn_q)
    small[:, S_K:S_K + KC] = columns(L0_attn_k)
    small[:, S_NW:S_NW + KC] = columns(L0_attn_norm_weight)
    small[:, S_LD:S_LD + KC] = columns(np.repeat(np.asarray(L0_attn_log_decay), DIM // 16))
    small[:, S_EB:S_END] = np.asarray(L0_ffn_expert_bias)[None, :]
    arrays = {
        "x": x.reshape(TOKENS, DIM),
        "small": small,
        "w_gate": np.asarray(L0_ffn_w_gate).T,
        "w_up": np.concatenate([np.asarray(L0_ffn_sw1).T, np.asarray(L0_ffn_sw3).T], axis=1),
        "w_down": np.asarray(L0_ffn_sw2).T,
        "w_o": np.asarray(L0_attn_o_w).T,
        "w1": np.asarray(L0_ffn_w1),
        "w2": np.asarray(L0_ffn_w2),
        "w3": np.asarray(L0_ffn_w3),
        "consts": constants(),
    }
    arrays = {n: np.ascontiguousarray(a) for n, a in arrays.items()}
    nc = bacc.Bacc("TRN2", target_bir_lowering=False, num_devices=1)
    args = [nc.dram_tensor(n, a.shape, mybir.dt.from_np(a.dtype), kind="ExternalInput").ap()
            for n, a in arrays.items()]
    out = nc.dram_tensor("out", (TOKENS, DIM), mybir.dt.float32, kind="ExternalOutput").ap()
    build(nc, *args, out)
    got = run_bass_kernel_spmd(nc, [arrays], core_ids=[0])
    return got.results[0]["out"].reshape(x.shape)
```

```python
import concourse.bass as bass
from concourse import mybir
from contextlib import ExitStack

P = 128
TOKENS, DIM = 8192, 256
KC = DIM // P
TILE = 512
HALF = TILE // 2
TT = TILE // P
NT = TOKENS // TILE
NB = NT // 2
NTT = TOKENS // P
E = 8
GRP = 4
HID = 128
TOPK = 2
ROWT = TOPK * NTT
FIRST_ROW_TILE = NT // 2
RPT = ROWT // (NT - FIRST_ROW_TILE)
ROW_TILES = NT - FIRST_ROW_TILE
RG = 4
PAIRS = E * E
LN_EPS, RMS_EPS = 1e-5, 1e-6
FAR = 1e38
LEAST = 1.1754944e-38

C_IDENT, C_HEADS, C_THR8, C_THR4, C_POS, C_IOTA, C_PAIR = 0, 128, 256, 320, 336, 464, 472
C_END = 473
S_Q, S_K, S_NW, S_LD, S_EB, S_END = 0, 2, 4, 6, 8, 16


def build(nc, x, small, w_gate, w_up, w_down, w_o, w1, w2, w3, consts, out):
    f32, f32r, bf16 = mybir.dt.float32, mybir.dt.float32r, mybir.dt.bfloat16
    ALU = mybir.AluOpType
    ACT = mybir.ActivationFunctionType
    AX = mybir.AxisListType
    V, G, A, T = nc.vector, nc.gpsimd, nc.scalar, nc.tensor

    x_v = x.rearrange("(n p) d -> p n d", p=P)
    out_v = out.rearrange("(n p) d -> p n d", p=P)
    codes_dram = nc.dram_tensor("row_codes", (ROWT, P), bf16, kind="Internal").ap()

    ctx = ExitStack()
    with ctx:
        def sb(name, shape, dt=f32):
            return ctx.enter_context(nc.sbuf_tensor(name, shape, dt))

        def bank(name):
            return ctx.enter_context(nc.psum_tensor(name, [P, 512], f32))

        def sem(name):
            return ctx.enter_context(nc.semaphore(name))

        x_sb = sb("x_sb", [P, NTT, DIM])
        e_sb = sb("e_sb", [P, KC, TOKENS])
        raw_up = e_sb[:, 0, 1024:2048].rearrange("p (k n) -> p k n", k=KC)
        raw_down = e_sb[:, 0, 2048:2560].rearrange("p (k n) -> p k n", k=KC)
        raw_o = e_sb[:, 0, 2560:3072].rearrange("p (k n) -> p k n", k=KC)
        raw_gate = e_sb[:, 0, 3072:3072 + KC * E].rearrange("p (k n) -> p k n", k=KC)
        w1_sb = e_sb[:, 0, 4096:6144].rearrange("p (k g h) -> p k g h", k=KC, g=E)
        w3_sb = e_sb[:, 1, 4096:6144].rearrange("p (k g h) -> p k g h", k=KC, g=E)
        w2_sb = e_sb[:, 0, 0:E * DIM].rearrange("p (g d) -> p g d", g=E)
        codes_bc = e_sb[:, 1, 0:RPT * P].bitcast(bf16).rearrange("p (u n) -> p u n", u=2)

        xn = sb("xn", [P, 2, TT, DIM])
        xh = sb("xh", [P, 2, KC, TILE], f32r)
        xl = sb("xl", [P, 2, KC, TILE], f32r)
        act_out = sb("act_out", [P, 2, TILE])
        hh = sb("hh", [P, 2, 2, TILE], f32r)
        hl = sb("hl", [P, 2, 2, TILE], f32r)
        sq = sb("sq", [P, KC, TILE])
        gate_rows = sq[0:2 * E, 1, :]
        pair_hot_t = [t[:, :, :, :].rearrange("p a b n -> p (a b n)") for t in (hh, hl)]
        pair_w = [xn[:, u, :, :].rearrange("p a (b g e) -> p (a b) g e", g=E, e=E) for u in (0, 1)]

        wup_h = sb("wup_h", [P, KC, 512], f32r)
        wup_l = sb("wup_l", [P, KC, 512], f32r)
        wdn_h = sb("wdn_h", [P, KC, DIM], f32r)
        wdn_l = sb("wdn_l", [P, KC, DIM], f32r)
        wo_h = sb("wo_h", [P, KC, DIM], f32r)
        wo_l = sb("wo_l", [P, KC, DIM], f32r)
        wg_hl = sb("wg_hl", [P, KC, 2, E], f32r)

        cst = sb("cst", [P, C_END])
        ident = cst[:, C_IDENT:C_IDENT + P]
        heads = cst[:, C_HEADS:C_HEADS + P]
        thr8 = cst[:, C_THR8:C_THR8 + 64].rearrange("p (j i) -> p j i", j=E)
        thr4 = cst[:, C_THR4:C_THR4 + 16].rearrange("p (j i) -> p j i", j=GRP)
        pos = cst[:, C_POS:C_POS + ROWT]
        iota = cst[:, C_IOTA:C_IOTA + E]
        pair_no = cst[:, C_PAIR:C_PAIR + 1]
        par = sb("par", [P, S_END])
        ones = sb("ones", [P, P])
        lam = sb("lam", [P, KC])
        qk = sb("qk", [P, KC])
        c_col = sb("c_col", [P, KC])
        o_scale = sb("o_scale", [P, KC])

        stats = sb("stats", [P, TT, 6])
        mean_var = sb("mean_var", [P, TT, 2])
        var_eps = sb("var_eps", [P, 2, TT])
        neg_mean = sb("neg_mean", [P, 2, TT])
        rstd = sb("rstd", [P, 2, TT])
        shift = sb("shift", [P, 2, TT])
        power = sb("power", [P, E])
        ms = sb("ms", [P, NTT])
        rms = sb("rms", [P, NTT])

        logit = sb("logit", [P, E, E])
        top = sb("top", [P, E])
        prob = sb("prob", [P, E, E])
        total = sb("total", [P, E])
        score = sb("score", [P, E, E])
        gscore = sb("gscore", [P, E, GRP])
        grank = sb("grank", [P, E, GRP])
        diff = sb("diff", [P, E, E, E])
        flat_diff = diff[:, :, :, :].rearrange("p t j i -> p (t j i)")
        gdiff = flat_diff[:, 0:E * GRP * GRP].rearrange("p (t j i) -> p t j i", t=E, j=GRP)
        scaled_pick = flat_diff[:, 0:2 * E * E].rearrange("p (r e) -> p r e", e=E)
        rank = sb("rank", [P, E, E])
        pick = sb("pick", [P, ROWT, E], bf16)
        pick_w = sb("pick_w", [P, ROWT, E])
        row_w = sb("row_w", [P, ROWT])
        row_e = sb("row_e", [P, ROWT])

        x8 = sb("x8", [P, KC, E])
        ab = sb("ab", [P, 3, PAIRS])
        a_hl = sb("a_hl", [P, HID], f32r)
        group_hot = sq[:, 0, :].bitcast(bf16).rearrange("p (j g) -> p j g", g=E)
        row_g = sq[:, 1, 0:ROWT]
        code = sq[:, 1, 128:128 + ROWT]
        a_t = sq[:, 1, 256:256 + HID]
        count = sb("count", [P, E])
        ends = sb("ends", [P, E])
        past = flat_diff.bitcast(bf16).rearrange("p (j g) -> p j g", g=E)
        code_t = sb("code_t", [P, P], bf16)
        row_w_now = sb("row_w_now", [P, 2, RPT])
        warm = sb("warm", [P, 1])
        s_sum = sb("s_sum", [P, PAIRS])

        tp = [bank("tp0"), bank("tp1")]
        up = [bank("up0"), bank("up1"), bank("up2")]
        dn = [bank("dn0"), bank("dn1")]
        misc = bank("misc")
        m_gate = misc[:, 0:2 * E * TT]
        m_ssq = misc[:, 176:176 + TT - 1 + 64]
        m_ab = misc[:, 256:256 + 2 * PAIRS + 7 * E]
        m_wide = misc[:, 384:512]
        att = [tp, dn]

        x_in = [sem("x_in0"), sem("x_in1")]
        small_in, bias_in, cst_in = sem("small_in"), sem("bias_in"), sem("cst_in")
        x_first = sem("x_first")
        up_in, gate_in, w13_in = sem("up_in"), sem("gate_in"), sem("w13_in")
        down_in, o_in = sem("down_in"), sem("o_in")
        w2_in = sem("w2_in")
        codes_out = sem("codes_out")
        codes_in = [sem("codes_in0"), sem("codes_in1")]
        stored = sem("stored")
        setup = sem("setup")
        decay_exp, power_set, qk_sum = sem("decay_exp"), sem("power_set"), sem("qk_sum")
        params = sem("params")
        o_scaled = sem("o_scaled")
        w_hi, w_lo = sem("w_hi"), sem("w_lo")
        stat_step = sem("stat_step")
        ln_stats = sem("ln_stats")
        rstd_step, rstd_ready = sem("rstd_step"), sem("rstd_ready")
        xn_ready = sem("xn_ready")
        tp_ready = sem("tp_ready")
        xh_ready, xl_ready = sem("xh_ready"), sem("xl_ready")
        e_ready = sem("e_ready")
        up_ready = sem("up_ready")
        silu_ready, h_ready = sem("silu_ready"), sem("h_ready")
        hh_ready, hl_ready = sem("hh_ready"), sem("hl_ready")
        sq_ready, sq_added = sem("sq_ready"), sem("sq_added")
        gate_ready, gate_sb = sem("gate_ready"), sem("gate_sb")
        misc_ready = sem("misc_ready")
        last_logits = sem("last_logits")
        ms_read, logit_read = sem("ms_read"), sem("logit_read")
        dn_ready, y_ready = sem("dn_ready"), sem("y_ready")
        route = sem("route")
        exp_ready = sem("exp_ready")
        rms_ready = sem("rms_ready")
        x8_ready, ab_read = sem("x8_ready"), sem("ab_read")
        eh_ready, el_ready = sem("eh_ready"), sem("el_ready")
        att_ready = sem("att_ready")
        o_ready = sem("o_ready")
        place = sem("place")
        count_ready, code_ready, code_tr = sem("count_ready"), sem("code_ready"), sem("code_tr")
        a_tr, a_ready = sem("a_tr"), sem("a_ready")
        code_sb = sem("code_sb")
        hot_ready, pair_w_ready = sem("hot_ready"), sem("pair_w_ready")
        roww_ready = sem("roww_ready")
        gathered = sem("gathered")
        row_silu = sem("row_silu")
        reduced = sem("reduced")
        s_added = sem("s_added")
        h_pairs, routed, first8_ready = sem("h_pairs"), sem("routed"), sem("first8_ready")

        ROUTE_STEPS = 21

        def token_tile(i, t):
            return x_sb[:, bass.ds(TT * i + t, 1), :].rearrange("p a d -> p (a d)")

        block = ctx.enter_context(nc.Block())

        @block.sync
        def _(sp):
            sp.dma_start(x_sb[:, 0:2, :], x_v[:, 0:2, :]).then_inc(x_first, 16)
            sp.dma_start(x_sb[:, 2:TT, :], x_v[:, 2:TT, :]).then_inc(x_in[0], 16)
            sp.dma_start(par[:, 0:S_EB], small[:, 0:S_EB]).then_inc(small_in, 16)
            sp.dma_start(x_sb[:, TT:2 * TT, :], x_v[:, TT:2 * TT, :]).then_inc(x_in[1], 16)
            for k in range(KC):
                sp.dma_start(w1_sb[:, k, :, :], w1[:, k * P:(k + 1) * P, :].rearrange("g p h -> p g h"))\
                    .then_inc(w13_in, 16)
                sp.dma_start(w3_sb[:, k, :, :], w3[:, k * P:(k + 1) * P, :].rearrange("g p h -> p g h"))\
                    .then_inc(w13_in, 16)
            sp.dma_start(raw_down, w_down.rearrange("(k p) n -> p k n", p=P)).then_inc(down_in, 16)
            sp.dma_start(raw_o, w_o.rearrange("(k p) n -> p k n", p=P)).then_inc(o_in, 16)
            sp.dma_start(par[:, S_EB:S_END], small[0:1, S_EB:S_END].to_broadcast([P, E])).then_inc(bias_in, 16)
            with sp.Fori(1, NB) as b:
                for u in range(2):
                    i = 2 * b + u
                    sp.wait_ge(x_in[u], 16 * b)
                    sp.dma_start(x_sb[:, bass.ds(TT * i, TT), :],
                                 x_v[:, bass.ds(TT * i, TT), :]).then_inc(x_in[u], 16)

            sp.wait_ge(o_ready, TT)
            sp.dma_start(out_v[E:P, 0, :], x_sb[E:P, 0, :]).then_inc(stored, 16)
            sp.dma_start(out_v[:, 1:TT, :], x_sb[:, 1:TT, :]).then_inc(stored, 16)

            def store(i):
                sp.wait_ge(o_ready, TT * i + TT)
                sp.dma_start(out_v[:, bass.ds(TT * i, TT), :],
                             x_sb[:, bass.ds(TT * i, TT), :]).then_inc(stored, 16)

            store(1)
            store(2)
            sp.wait_ge(eh_ready, 2 * 4)
            sp.wait_ge(el_ready, 2 * 4)
            sp.wait_ge(code_sb, 1)
            sp.dma_start(codes_dram, code_t[:, :]).then_inc(codes_out, 16)
            sp.wait_ge(codes_out, 16)
            for u in range(2):
                sp.dma_start(codes_bc[:, u, :], codes_dram[RPT * u:RPT * (u + 1), :]
                             .rearrange("(o j) n -> o (j n)", o=1).to_broadcast([P, RPT * P]))\
                    .then_inc(codes_in[u], 16)
            with sp.Fori(3, FIRST_ROW_TILE) as i:
                store(i)
            sp.dma_start(w2_sb, w2.rearrange("g h d -> h g d")).then_inc(w2_in, 16)
            with sp.Fori(0, (NT - FIRST_ROW_TILE) // 2 - 1) as b:
                for u in range(2):
                    i = FIRST_ROW_TILE + 2 * b + u
                    sp.wait_ge(hot_ready, 2 * b + u + 1)
                    sp.dma_start(codes_bc[:, u, :],
                                 codes_dram[bass.ds(RPT * (2 * b + u + 2), RPT), :]
                                 .rearrange("(o j) n -> o (j n)", o=1).to_broadcast([P, RPT * P]))\
                        .then_inc(codes_in[u], 16)
                    store(i)
            store(NT - 2)
            store(NT - 1)
            sp.wait_ge(first8_ready, 1)
            sp.dma_start(out[0:E, :], x_sb[0:E, 0, :]).then_inc(stored, 16)
            sp.wait_ge(stored, 16 * (NT + 2))

        @block.gpsimd
        def _(pool):
            G.memset(power[:, :], -0.5).then_inc(power_set, 1)
            pool.wait_ge(power_set, 1)

            def token_scale(i, u):
                pool.wait_ge(ln_stats, 2 * i + 2)
                if not (isinstance(i, int) and i < 2):
                    pool.wait_ge(xn_ready, TT * (i - 1))
                G.tensor_tensor(rstd[:, u, :], var_eps[:, u, :], power[:, 0:TT], ALU.pow).then_inc(rstd_step, 1)
                pool.wait_ge(rstd_step, i + 1)
                G.tensor_tensor(shift[:, u, :], neg_mean[:, u, :], rstd[:, u, :], ALU.mult).then_inc(rstd_ready, 1)

            def sum_squares(i):
                pool.wait_ge(sq_ready, 2 * i + 2)
                G.tensor_tensor(sq[:, 0, :], sq[:, 0, :], sq[:, 1, :], ALU.add).then_inc(sq_added, 1)

            def h_lo(i, u, m):
                pool.wait_ge(hh_ready, 2 * i + m + 1)
                G.tensor_tensor(hl[:, u, m, :], act_out[:, m, :], hh[:, u, m, :].bitcast(f32),
                                ALU.subtract).then_inc(hl_ready, 1)

            def rms_factors(b):
                pool.wait_ge(ms_read, 2 * b + 2)
                at = bass.ds(E * b, E)
                G.tensor_tensor(rms[:, at], ms[:, at], power[:, :], ALU.pow).then_inc(rms_ready, 1)

            def batch(b, first=False, last=False):
                for u in range(2):
                    i = 2 * b + u
                    if not (first and u == 0):
                        sum_squares(i - 1)
                    h_lo(i, u, 0)
                    if u == 1 and not first:
                        rms_factors(b - 1)
                    if not last:
                        token_scale(i + 2, u)
                    elif u == 1:
                        e_lo(0, 0)
                    h_lo(i, u, 1)

            def e_lo(i, u):
                for h in range(2):
                    half = slice(h * HALF, (h + 1) * HALF)
                    pool.wait_ge(eh_ready, 2 * i + h + 1)
                    G.tensor_tensor(xl[:, u, :, half], e_sb[:, :, bass.ds(TILE * i + h * HALF, HALF)],
                                    xh[:, u, :, half].bitcast(f32), ALU.subtract).then_inc(el_ready, 1)

            def weight_lo(lo, hi, raw, n):
                pool.wait_ge(w_hi, n)
                G.tensor_tensor(lo, raw, hi.bitcast(f32), ALU.subtract).then_inc(w_lo, 1)

            token_scale(0, 0)
            weight_lo(wup_l[:, :, :], wup_h[:, :, :], raw_up, 1)
            token_scale(1, 1)
            weight_lo(wg_hl[:, :, 1, :], wg_hl[:, :, 0, :], raw_gate, 2)
            weight_lo(wdn_l[:, :, :], wdn_h[:, :, :], raw_down, 3)
            weight_lo(wo_l[:, :, :], wo_h[:, :, :], raw_o, 4)
            batch(0, first=True)
            with pool.Fori(1, NB - 1) as b:
                batch(b)
            batch(NB - 1, last=True)
            e_lo(1, 1)
            sum_squares(NT - 1)
            e_lo(2, 0)
            rms_factors(NB - 1)
            e_lo(3, 1)
            with pool.Fori(2, NB) as b:
                for u in range(2):
                    e_lo(2 * b + u, u)

        @block.scalar
        def _(act):
            act.dma_start(raw_up, w_up.rearrange("(k p) n -> p k n", p=P)).then_inc(up_in, 16)
            act.dma_start(raw_gate, w_gate.rearrange("(k p) n -> p k n", p=P)).then_inc(gate_in, 16)
            act.dma_start(cst[:, :], consts).then_inc(cst_in, 16)
            act.wait_ge(small_in, 16)
            A.activation(lam[:, :], par[:, S_LD:S_LD + KC], ACT.Exp, scale=-1.0).then_inc(decay_exp, 1)

            def normalize(i, u):
                act.wait_ge(rstd_ready, i + 1)
                if not (isinstance(i, int) and i < 2):
                    act.wait_ge(tp_ready, 2 * i - 2)
                for t in range(TT):
                    A.activation(xn[:, u, t, :], token_tile(i, t), ACT.Identity, bias=shift[:, u, t:t + 1],
                                 scale=rstd[:, u, t:t + 1]).then_inc(xn_ready, 1)

            def x_hi(i, u):
                for k in range(KC):
                    act.wait_ge(tp_ready, 2 * i + k + 1)
                    A.activation(xh[:, u, k, :], tp[k][:, :], ACT.Copy).then_inc(xh_ready, 1)

            def silu(i, m, first=False):
                act.wait_ge(up_ready, 4 * i + 2 * m + 1)
                if not first:
                    act.wait_ge(hl_ready, 2 * i + m - 1)
                A.activation(act_out[:, m, :], up[2 * m][:, :], ACT.Silu).then_inc(silu_ready, 1)

            def h_hi(i, u, m, first=False):
                act.wait_ge(h_ready, 2 * i + m + 1)
                if not first:
                    act.wait_ge(dn_ready, 2 * i - 2)
                A.activation(hh[:, u, m, :], act_out[:, m, :], ACT.Copy).then_inc(hh_ready, 1)

            def gate_copy(i):
                act.wait_ge(gate_ready, i + 1)
                if not (isinstance(i, int) and i == 0):
                    act.wait_ge(sq_added, i)
                A.activation(gate_rows, up[1][0:2 * E, :], ACT.Copy).then_inc(gate_sb, 1)

            def squares(i, first=False):
                act.wait_ge(e_ready, 2 * i + 2)
                act.wait_ge(misc_ready, i + 1)
                for k in range(KC):
                    A.activation(sq[:, k, :], e_sb[:, k, bass.ds(TILE * i, TILE)], ACT.Square,
                                 scale=c_col[:, k:k + 1]).then_inc(sq_ready, 1)

            def router_exp(b):
                act.wait_ge(route, ROUTE_STEPS * b + 2)
                A.activation(prob[:, :, :], prob[:, :, :], ACT.Exp).then_inc(exp_ready, 1)

            def batch(b, first=False, last=False):
                for u in range(2):
                    i = 2 * b + u
                    silu(i, 0, first and u == 0)
                    if not (first and u == 0):
                        squares(i - 1, first)
                    if last and u == 1:
                        act.wait_ge(misc_ready, NT - 1)
                        e_hi_half(0, 0, 0)
                        e_hi_half(0, 0, 1)
                    else:
                        x_hi(i + 1, 1 - u)
                    if u == 0 and not first:
                        router_exp(b - 1)
                    else:
                        h_hi(i, u, 0, first)
                    silu(i, 1, first and u == 0)
                    if u == 0 and not first:
                        h_hi(i, u, 0)
                    gate_copy(i)
                    h_hi(i, u, 1, first)
                    if not last:
                        normalize(i + 2, u)
                    elif u == 1:
                        router_exp(b)

            def e_hi_half(i, u, h):
                A.activation(xh[:, u, :, h * HALF:(h + 1) * HALF], e_sb[:, :, bass.ds(TILE * i + h * HALF, HALF)],
                             ACT.Copy).then_inc(eh_ready, 1)

            def e_hi(i, u, h):
                act.wait_ge(att_ready, 2 * i + h - 3)
                e_hi_half(i, u, h)

            def weight_hi(hi, raw):
                A.activation(hi, raw, ACT.Copy).then_inc(w_hi, 1)

            act.wait_ge(up_in, 16)
            weight_hi(wup_h[:, :, :], raw_up)
            normalize(0, 0)
            x_hi(0, 0)
            act.wait_ge(gate_in, 16)
            weight_hi(wg_hl[:, :, 0, :], raw_gate)
            normalize(1, 1)
            act.wait_ge(down_in, 16)
            weight_hi(wdn_h[:, :, :], raw_down)
            act.wait_ge(o_in, 16)
            act.wait_ge(params, 1)
            for k in range(KC):
                A.activation(raw_o[:, k, :], raw_o[:, k, :], ACT.Copy, scale=o_scale[:, k:k + 1])\
                    .then_inc(o_scaled, 1)
            act.wait_ge(o_scaled, KC)
            weight_hi(wo_h[:, :, :], raw_o)
            batch(0, first=True)
            with act.Fori(1, NB - 1) as b:
                batch(b)
            batch(NB - 1, last=True)
            act.wait_ge(last_logits, 1)
            e_hi_half(1, 1, 0)
            e_hi_half(1, 1, 1)
            squares(NT - 1)
            with act.Fori(1, FIRST_ROW_TILE // 2) as b:
                for u in range(2):
                    for h in range(2):
                        e_hi(2 * b + u, u, h)

            e_hi(FIRST_ROW_TILE, 0, 0)
            e_hi(FIRST_ROW_TILE, 0, 1)
            A.activation(warm[:, :], ones[:, 0:1], ACT.Silu)

            def rows(n, u, last=False):
                if not last:
                    e_hi(FIRST_ROW_TILE + n + 1, 1 - u, 0)
                    e_hi(FIRST_ROW_TILE + n + 1, 1 - u, 1)
                act.wait_ge(roww_ready, n + 1)
                for q in range(RPT // RG):
                    act.wait_ge(gathered, (RPT // RG) * n + q + 1)
                    if q >= 2:
                        act.wait_ge(reduced, (RPT // RG) * n + q - 1)
                    for r in range(RG):
                        j = RG * q + r
                        A.activation(act_out[:, q % 2, r * HID:(r + 1) * HID],
                                     up[q % 2][:, r * HID:(r + 1) * HID], ACT.Silu,
                                     scale=row_w_now[:, u, j:j + 1]).then_inc(row_silu, 1)

            with act.Fori(0, ROW_TILES // 2 - 1) as b:
                rows(2 * b, 0)
                rows(2 * b + 1, 1)
            rows(ROW_TILES - 2, 0)
            rows(ROW_TILES - 1, 1, last=True)

        @block.vector
        def _(dve):
            at_setup = 0

            def done(ins):
                nonlocal at_setup
                at_setup += 1
                ins.then_inc(setup, 1)
                dve.wait_ge(setup, at_setup)

            def bn(i, tiles=range(TT)):
                for t in tiles:
                    V.bn_stats(stats[:, t, :], token_tile(i, t)).then_inc(stat_step, 1)

            def wait_bn(i):
                dve.wait_ge(stat_step, 2 * TT * i + TT)

            def aggregate(i):
                for t in range(TT):
                    V.bn_aggr(mean_var[:, t, :], stats[:, t, :]).then_inc(stat_step, 1)

            def finish_stats(i, u):
                dve.wait_ge(stat_step, 2 * TT * i + 2 * TT)
                if not (isinstance(i, int) and i < 2):
                    dve.wait_ge(rstd_ready, i - 1)
                V.tensor_scalar(var_eps[:, u, :], mean_var[:, :, 1], LN_EPS, None, ALU.add).then_inc(ln_stats, 1)
                V.tensor_scalar(neg_mean[:, u, :], mean_var[:, :, 0], -1.0, None, ALU.mult).then_inc(ln_stats, 1)

            def x_lo(i, u, k):
                dve.wait_ge(xh_ready, 2 * i + k + 1)
                V.tensor_tensor(xl[:, u, k, :], tp[k][:, :], xh[:, u, k, :].bitcast(f32),
                                ALU.subtract).then_inc(xl_ready, 1)

            def scan(i, u, k):
                if u:
                    dve.wait_ge(e_ready, 2 * i + k - 1)
                start = e_sb[:, k, bass.ds(TILE * i - 1, 1)] if u else 0.0
                V.tensor_tensor_scan(e_sb[:, k, bass.ds(TILE * i, TILE)], lam[:, k:k + 1].to_broadcast([P, TILE]),
                                     tp[k][:, :], start, ALU.mult, ALU.add).then_inc(e_ready, 1)

            def gate_mul(i, m):
                dve.wait_ge(silu_ready, 2 * i + m + 1)
                dve.wait_ge(up_ready, 4 * i + 2 * m + 2)
                V.tensor_tensor(act_out[:, m, :], act_out[:, m, :], up[1 - m][:, :], ALU.mult).then_inc(h_ready, 1)

            def add_shared(i, a):
                dve.wait_ge(dn_ready, 2 * i + a + 1)
                at = x_sb[:, bass.ds(TT * i + 2 * a, 2), :]
                V.tensor_tensor(at, dn[a][:, :].rearrange("p (t d) -> p t d", t=2), at, ALU.add).then_inc(y_ready, 1)

            def read_mean_square(i):
                dve.wait_ge(misc_ready, i + 2)
                V.tensor_scalar(ms[:, bass.ds(TT * i, TT)], m_ssq[:, 0:TT], 1.0 / DIM, RMS_EPS, ALU.mult, ALU.add)\
                    .then_inc(ms_read, 1)

            def read_logits(i, u, last=False):
                if last:
                    dve.wait_ge(last_logits, 1)
                else:
                    dve.wait_ge(misc_ready, i + 1)
                V.tensor_reduce(logit[:, TT * u:TT * u + TT, :],
                                m_gate.rearrange("p (t h e) -> p t e h", h=2, e=E), AX.X,
                                ALU.add).then_inc(logit_read, 1)

            def after(b, n):
                dve.wait_ge(route, ROUTE_STEPS * b + n)

            def over_experts(t):
                return t[:, :].unsqueeze(2).to_broadcast([P, E, E])

            def route_max(b):
                dve.wait_ge(logit_read, 2 * b + 2)
                V.tensor_reduce(top[:, :], logit[:, :, :], AX.X, ALU.max).then_inc(route, 1)

            def route_shift(b):
                after(b, 1)
                V.tensor_tensor(prob[:, :, :], logit[:, :, :], over_experts(top), ALU.subtract).then_inc(route, 1)

            def route_total(b):
                dve.wait_ge(exp_ready, b + 1)
                V.tensor_reduce(total[:, :], prob[:, :, :], AX.X, ALU.add).then_inc(route, 1)

            def route_invert(b):
                after(b, 3)
                V.reciprocal(total[:, :], total[:, :]).then_inc(route, 1)

            def route_prob(b):
                after(b, 4)
                V.tensor_tensor(prob[:, :, :], prob[:, :, :], over_experts(total), ALU.mult).then_inc(route, 1)

            def route_score(b):
                after(b, 5)
                V.tensor_tensor(score[:, :, :], prob[:, :, :],
                                par[:, S_EB:S_END].unsqueeze(1).to_broadcast([P, E, E]), ALU.add).then_inc(route, 1)

            score_pairs = score[:, :, :].rearrange("p t (g h) -> p t g h", h=2)

            def route_group_score(b):
                after(b, 6)
                V.tensor_tensor(gscore[:, :, :], score_pairs[:, :, :, 0], score_pairs[:, :, :, 1],
                                ALU.add).then_inc(route, 1)

            def route_group_diff(b):
                after(b, 7)
                V.tensor_tensor(gdiff, gscore[:, :, :].unsqueeze(2).to_broadcast([P, E, GRP, GRP]),
                                gscore[:, :, :].unsqueeze(3).to_broadcast([P, E, GRP, GRP]),
                                ALU.subtract).then_inc(route, 1)

            def route_group_before(b):
                after(b, 8)
                V.tensor_tensor(gdiff, gdiff, thr4.unsqueeze(1).to_broadcast([P, E, GRP, GRP]),
                                ALU.is_ge).then_inc(route, 1)

            def route_group_rank(b):
                after(b, 9)
                V.tensor_reduce(grank[:, :, :], gdiff, AX.X, ALU.add).then_inc(route, 1)

            def route_group_penalty(b):
                after(b, 10)
                V.tensor_scalar(grank[:, :, :], grank[:, :, :], 1.5, -FAR, ALU.is_gt, ALU.mult).then_inc(route, 1)

            def route_mask(b):
                after(b, 11)
                V.tensor_tensor(score_pairs, score_pairs,
                                grank[:, :, :].unsqueeze(3).to_broadcast([P, E, GRP, 2]), ALU.add).then_inc(route, 1)

            def route_diff(b):
                after(b, 12)
                V.tensor_tensor(diff[:, :, :, :], score[:, :, :].unsqueeze(2).to_broadcast([P, E, E, E]),
                                score[:, :, :].unsqueeze(3).to_broadcast([P, E, E, E]), ALU.subtract).then_inc(route, 1)

            def route_before(b):
                after(b, 13)
                V.tensor_tensor(diff[:, :, :, :], diff[:, :, :, :],
                                thr8.unsqueeze(1).to_broadcast([P, E, E, E]), ALU.is_ge).then_inc(route, 1)

            def route_rank(b):
                after(b, 14)
                V.tensor_reduce(rank[:, :, :], diff[:, :, :, :], AX.X, ALU.add).then_inc(route, 1)

            def rows_of(b):
                return bass.ds(2 * E * b, 2 * E)

            def choices(t, b):
                return t[:, rows_of(b), :].rearrange("p (t k) e -> p t k e", k=TOPK)

            def route_pick(b):
                after(b, 15)
                for k in range(TOPK):
                    V.tensor_scalar(choices(pick, b)[:, :, k, :], rank[:, :, :], float(k), None,
                                    ALU.is_equal).then_inc(route, 1)

            def route_pick_weight(b):
                after(b, 17)
                V.tensor_tensor(choices(pick_w, b), choices(pick, b),
                                prob[:, :, :].unsqueeze(2).to_broadcast([P, E, TOPK, E]), ALU.mult).then_inc(route, 1)

            def route_pick_number(b):
                after(b, 17)
                V.tensor_tensor(scaled_pick, pick[:, rows_of(b), :],
                                iota.unsqueeze(1).to_broadcast([P, 2 * E, E]), ALU.mult).then_inc(route, 1)

            def route_row_weight(b):
                after(b, 18)
                V.tensor_reduce(row_w[:, rows_of(b)], pick_w[:, rows_of(b), :], AX.X, ALU.add).then_inc(route, 1)

            def route_row_expert(b):
                after(b, 19)
                V.tensor_reduce(row_e[:, rows_of(b)], scaled_pick, AX.X, ALU.add).then_inc(route, 1)

            V.memset(ones[:, :], 1.0)
            V.memset(s_sum[:, :], 0.0).then_inc(s_added, 1)
            dve.wait_ge(x_first, 16)
            bn(0, (0, 1))
            dve.wait_ge(x_in[0], 16)
            bn(0, (2, 3))
            wait_bn(0)
            aggregate(0)
            finish_stats(0, 0)
            dve.wait_ge(small_in, 16)
            done(V.tensor_tensor(qk[:, :], par[:, S_Q:S_Q + KC], par[:, S_K:S_K + KC], ALU.mult))
            dve.wait_ge(decay_exp, 1)
            done(V.tensor_scalar(lam[:, :], lam[:, :], 1.0, None, ALU.add))
            done(V.reciprocal(lam[:, :], lam[:, :]))
            dve.wait_ge(x_in[1], 16)
            bn(1)
            wait_bn(1)
            aggregate(1)
            finish_stats(1, 1)
            for k in range(KC):
                x_lo(0, 0, k)
            for k in range(KC):
                V.tensor_copy(x8[:, k, :], tp[k][:, 0:E]).then_inc(x8_ready, 1)
            for k in range(KC):
                scan(0, 0, k)
            dve.wait_ge(qk_sum, 1)
            done(V.tensor_copy(c_col[:, :], m_wide[:, 0:KC]))
            V.tensor_tensor(o_scale[:, :], c_col[:, :], par[:, S_NW:S_NW + KC], ALU.mult).then_inc(params, 1)
            dve.wait_ge(bias_in, 16)

            def read_tables():
                dve.wait_ge(misc_ready, 1)
                for a in range(2):
                    V.tensor_copy(ab[:, a, :], m_ab[:, 0:PAIRS]).then_inc(ab_read, 1)
                V.tensor_copy(ab[:, 2, :], m_ab[:, PAIRS:2 * PAIRS]).then_inc(ab_read, 1)

            def batch(b, first=False, last=False):
                r = b - 1
                i = 2 * b
                if not first:
                    read_mean_square(i - 2)
                    read_logits(i - 1, 1)
                    add_shared(i - 2, 0)
                    route_max(r)
                    add_shared(i - 2, 1)
                    route_shift(r)
                gate_mul(i, 0)
                if not last:
                    dve.wait_ge(x_in[0], 16 * (b + 2))
                    bn(i + 2)
                    wait_bn(i + 2)
                x_lo(i + 1, 1, 0)
                if not last:
                    aggregate(i + 2)
                    finish_stats(i + 2, 0)
                x_lo(i + 1, 1, 1)
                gate_mul(i, 1)
                scan(i + 1, 1, 0)
                scan(i + 1, 1, 1)

                if first:
                    read_tables()

                i = 2 * b + 1
                if not first:
                    read_mean_square(i - 2)
                read_logits(i - 1, 0)
                if not first:
                    add_shared(i - 2, 0)
                    route_total(r)
                    add_shared(i - 2, 1)
                    route_invert(r)
                    route_prob(r)
                gate_mul(i, 0)
                if not last:
                    dve.wait_ge(x_in[1], 16 * (b + 2))
                    bn(i + 2)
                    wait_bn(i + 2)
                if not first:
                    route_score(r)
                if not last:
                    aggregate(i + 2)
                if not first:
                    route_group_score(r)
                if not last:
                    finish_stats(i + 2, 1)
                    x_lo(i + 1, 0, 0)
                if not first:
                    route_group_diff(r)
                if not last:
                    x_lo(i + 1, 0, 1)
                if not first:
                    route_group_before(r)
                if not last:
                    scan(i + 1, 0, 0)
                if not first:
                    route_group_rank(r)
                if not last:
                    scan(i + 1, 0, 1)
                if not first:
                    route_group_penalty(r)
                if not last:
                    gate_mul(i, 1)
                if not first:
                    route_mask(r)
                    route_diff(r)
                    route_before(r)
                    route_rank(r)
                    route_pick(r)
                    route_pick_weight(r)
                    route_pick_number(r)
                    route_row_weight(r)
                    route_row_expert(r)
                if last:
                    gate_mul(i, 1)

            batch(0, first=True)
            with dve.Fori(1, NB - 1) as b:
                batch(b)
            batch(NB - 1, last=True)
            def add_attention(i, u, tiles=range(TT)):
                for t in tiles:
                    if t % 2 == 0:
                        dve.wait_ge(att_ready, 2 * i + t // 2 + 1)
                    at = token_tile(i, t)
                    V.scalar_tensor_tensor(at, att[u][t // 2][:, (t % 2) * DIM:(t % 2 + 1) * DIM],
                                           rms[:, bass.ds(TT * i + t, 1)], at, ALU.mult, ALU.add).then_inc(o_ready, 1)

            last = NB - 1
            read_logits(NT - 1, 1, last=True)
            route_max(last)
            route_shift(last)
            add_shared(NT - 2, 0)
            add_shared(NT - 2, 1)
            route_total(last)
            read_mean_square(NT - 2)
            route_invert(last)
            route_prob(last)
            route_score(last)
            route_group_score(last)
            route_group_diff(last)
            route_group_before(last)
            route_group_rank(last)
            route_group_penalty(last)
            dve.wait_ge(rms_ready, NB - 1)
            add_attention(0, 0, (0,))
            route_mask(last)
            add_shared(NT - 1, 0)
            route_diff(last)
            add_shared(NT - 1, 1)
            route_before(last)
            add_attention(0, 0, (1,))
            route_rank(last)
            add_attention(0, 0, (2,))
            route_pick(last)
            add_attention(0, 0, (3,))
            read_mean_square(NT - 1)
            dve.wait_ge(route, ROUTE_STEPS * NB - 4)
            V.tensor_reduce(count[:, :], pick[:, :, :].rearrange("p j e -> p e j"), AX.X, ALU.add).then_inc(place, 1)
            route_pick_weight(last)
            route_pick_number(last)
            add_attention(1, 1, (0,))
            route_row_weight(last)
            add_attention(1, 1, (1,))
            route_row_expert(last)
            dve.wait_ge(count_ready, 1)
            V.tensor_tensor_scan(ends[:, :], ones[:, 0:E], m_wide[:, 0:E], 0.0, ALU.mult, ALU.add).then_inc(place, 1)
            add_attention(1, 1, (2,))
            dve.wait_ge(place, 2)
            V.tensor_tensor(past, pos.unsqueeze(2).to_broadcast([P, ROWT, E]),
                            ends[:, :].unsqueeze(1).to_broadcast([P, ROWT, E]), ALU.is_ge).then_inc(place, 1)
            add_attention(1, 1, (3,))
            dve.wait_ge(place, 3)
            V.tensor_reduce(row_g, past, AX.X, ALU.add).then_inc(place, 1)
            add_attention(2, 0, (0,))
            dve.wait_ge(place, 4)
            V.scalar_tensor_tensor(code, row_g, float(E), row_e[:, :], ALU.mult, ALU.add)\
                .then_inc(code_ready, 1)
            add_attention(2, 0, (1, 2))
            dve.wait_ge(code_tr, 1)
            V.tensor_copy(code_t[:, :], m_wide).then_inc(code_sb, 1)
            add_attention(2, 0, (3,))
            add_attention(3, 1)
            V.tensor_tensor(group_hot, row_g.unsqueeze(2).to_broadcast([P, ROWT, E]),
                            iota.unsqueeze(1).to_broadcast([P, ROWT, E]), ALU.is_equal).then_inc(place, 1)
            dve.wait_ge(a_tr, 1)
            V.tensor_copy(a_t, m_wide).then_inc(place, 1)
            V.tensor_copy(a_hl[:, :], m_wide).then_inc(place, 1)
            add_attention(4, 0)
            dve.wait_ge(place, 7)
            V.tensor_tensor(a_hl[PAIRS:P, :], a_t[PAIRS:P, :], a_hl[PAIRS:P, :].bitcast(f32), ALU.subtract)\
                .then_inc(a_ready, 1)
            dve.wait_ge(rms_ready, NB)

            def row_operands(n, u, turn):
                rows = bass.ds(RPT * n, RPT)
                dve.wait_ge(codes_in[u], 16 * turn + 16)
                V.tensor_scalar(pair_hot_t[u].bitcast(f32r), codes_bc[:, u, :], pair_no, None,
                                ALU.is_equal).then_inc(hot_ready, 1)
                V.tensor_copy(row_w_now[:, u, :], row_w[:, rows]).then_inc(roww_ready, 1)
                V.tensor_tensor(pair_w[u], group_hot[:, rows, :].unsqueeze(3).to_broadcast([P, RPT, E, E]),
                                pick_w[:, rows, :].unsqueeze(2).to_broadcast([P, RPT, E, E]),
                                ALU.mult).then_inc(pair_w_ready, 1)

            def add_pair_sums(n):
                dve.wait_ge(reduced, (RPT // RG) * (n + 1))
                dve.wait_ge(s_added, n + 1)
                V.tensor_tensor(s_sum[:, :], s_sum[:, :], up[2][:, 0:PAIRS], ALU.add).then_inc(s_added, 1)

            add_attention(5, 1)
            add_attention(6, 0)
            row_operands(0, 0, 0)
            add_attention(7, 1)
            with dve.Fori(0, ROW_TILES // 2 - 1) as b:
                row_operands(2 * b + 1, 1, b)
                add_attention(FIRST_ROW_TILE + 2 * b, 0)
                add_pair_sums(2 * b)
                row_operands(2 * b + 2, 0, b + 1)
                add_attention(FIRST_ROW_TILE + 2 * b + 1, 1)
                add_pair_sums(2 * b + 1)
            row_operands(ROW_TILES - 1, 1, ROW_TILES // 2 - 1)
            add_attention(NT - 2, 0)
            add_pair_sums(ROW_TILES - 2)
            add_attention(NT - 1, 1)
            add_pair_sums(ROW_TILES - 1)
            dve.wait_ge(s_added, NT - FIRST_ROW_TILE + 1)
            V.tensor_tensor(s_sum[:, :], s_sum[:, :], ab[:, 2, :], ALU.mult).then_inc(h_pairs, 1)
            dve.wait_ge(routed, 1)
            V.tensor_tensor(x_sb[0:E, 0, :], x_sb[0:E, 0, :], misc[0:E, 0:DIM], ALU.add).then_inc(first8_ready, 1)

        @block.tensor
        def _(pe):
            def parts(w_h, w_l, a_h, a_l):
                return [(w_h, a_h), (w_l, a_h), (w_h, a_l)]

            def first_transposes():
                for t in range(TT):
                    pe.wait_ge(xn_ready, t + 1)
                    for k in range(KC):
                        last = T.transpose(tp[k][:, t * P:(t + 1) * P], xn[:, 0, t, k * P:(k + 1) * P], ident)
                        if t == TT - 1:
                            last.then_inc(tp_ready, 1)

            def transposes(i, u):
                pe.wait_ge(xn_ready, TT * i + TT)
                pe.wait_ge(e_ready, 2 * i)
                for k in range(KC):
                    for t in range(TT):
                        last = T.transpose(tp[k][:, t * P:(t + 1) * P], xn[:, u, t, k * P:(k + 1) * P], ident)
                    last.then_inc(tp_ready, 1)

            def up_half(i, u, m, first=False):
                for n in range(2):
                    if m == 0 and n == 0:
                        if not first:
                            pe.wait_ge(h_ready, 2 * i)
                            pe.wait_ge(gate_sb, i)
                    if m == 1 and n == 1:
                        pe.wait_ge(silu_ready, 2 * i + 1)
                    to = up[(2 * m + n) % 3]
                    cols = slice(n * DIM + m * P, n * DIM + (m + 1) * P)
                    run = [(w[:, k, cols], a[:, u, k, :]) for w, a in parts(wup_h, wup_l, xh, xl) for k in range(KC)]
                    for j, (w, a) in enumerate(run):
                        last = T.matmul(to[:, :], w, a, start=(j == 0), stop=(j == len(run) - 1))
                    last.then_inc(up_ready, 1)

            def gate(i, u):
                pe.wait_ge(h_ready, 2 * i + 1)
                run = [(wg_hl[:, k, :, :].rearrange("p h e -> p (h e)"), a[:, u, k, :])
                       for a in (xh, xl) for k in range(KC)]
                for j, (w, a) in enumerate(run):
                    last = T.matmul(up[1][0:2 * E, :], w, a, start=(j == 0), stop=(j == len(run) - 1))
                last.then_inc(gate_ready, 1)

            def gate_transposes():
                for t in range(TT):
                    last = T.transpose(m_gate[:, 2 * E * t:2 * E * t + 2 * E], gate_rows[:, t * P:(t + 1) * P],
                                       ident[0:2 * E, 0:2 * E])
                return last

            def square_sum(t):
                return T.matmul(m_ssq[:, t:t + 64], sq[:, 0, t * P:(t + 1) * P], ones[:, 0:64], start=True, stop=True)

            def wait_down(i, first=False):
                if first:
                    pe.wait_ge(w_lo, 3)
                pe.wait_ge(hl_ready, 2 * i + 2)
                if not first:
                    pe.wait_ge(y_ready, 2 * i)

            def down(u, t):
                tok = slice(t * P, (t + 1) * P)
                run = [(a[:, u, k, tok], w[:, k, :]) for w, a in parts(wdn_h, wdn_l, hh, hl) for k in range(KC)]
                for j, (a, w) in enumerate(run):
                    last = T.matmul(dn[t // 2][:, (t % 2) * DIM:(t % 2 + 1) * DIM], a, w,
                                    start=(j == 0), stop=(j == len(run) - 1))
                if t % 2:
                    last.then_inc(dn_ready, 1)

            def tables():
                pe.wait_ge(w13_in, 64)
                pe.wait_ge(x8_ready, 2)
                for a, w in enumerate((w1_sb, w3_sb)):
                    for g in range(E):
                        for k in range(KC):
                            at = PAIRS * a + E * g
                            T.matmul(m_ab[:, at:at + 8 * E].rearrange("p (r n) -> p r n", r=8), w[:, k, g, :],
                                     x8[:, k, :].unsqueeze(1).to_broadcast([P, 8, E]),
                                     start=(k == 0), stop=(k == KC - 1))

            def squares_sum(i):
                pe.wait_ge(sq_added, i + 1)
                for t in range(TT):
                    done = square_sum(t)
                done.then_inc(misc_ready, 1)

            def last_tile():
                gate(NT - 1, 1)
                wait_down(NT - 2)
                down(0, 0)
                pe.wait_ge(gate_sb, NT)
                pe.wait_ge(logit_read, NT - 1)
                down(0, 1)
                gate_transposes().then_inc(last_logits, 1)
                down(0, 2)
                down(0, 3)
                pe.wait_ge(logit_read, NT)
                squares_sum(NT - 2)

            def batch(b, first=False, last=False):
                for u in range(2):
                    i = 2 * b + u
                    up_half(i, u, 0, first and u == 0)
                    if not (last and u == 1):
                        transposes(i + 1, 1 - u)
                    up_half(i, u, 1)
                    if last and u == 1:
                        last_tile()
                        break
                    if first and u == 0:
                        pe.wait_ge(w_lo, 2)
                    gate(i, u)
                    if first and u == 0:
                        pe.wait_ge(setup, 4)
                        tables()
                        pe.wait_ge(gate_sb, 1)
                        done = gate_transposes()
                    else:
                        wait_down(i - 1, first)
                        for t in range(TT):
                            if t == TT - 1:
                                pe.wait_ge(gate_sb, i + 1)
                                pe.wait_ge(logit_read, i)
                                if first:
                                    pe.wait_ge(ab_read, 3)
                            down(1 - u, t)
                        gate_transposes()
                        pe.wait_ge(sq_added, i)
                        for t in range(TT):
                            done = square_sum(t)
                    done.then_inc(misc_ready, 1)

            pe.wait_ge(cst_in, 16)
            pe.wait_ge(setup, 1)
            T.matmul(m_wide[:, 0:KC], heads, qk[:, :], start=True, stop=True).then_inc(qk_sum, 1)
            first_transposes()
            pe.wait_ge(w_lo, 1)
            pe.wait_ge(xl_ready, 2)
            batch(0, first=True)
            with pe.Fori(1, NB - 1) as b:
                batch(b)
            batch(NB - 1, last=True)

            def attention(i, u, tiles=range(TT)):
                for t in tiles:
                    if t % 2 == 0:
                        pe.wait_ge(el_ready, 2 * i + t // 2 + 1)
                    tok = slice(t * P, (t + 1) * P)
                    run = [(a[:, u, k, tok], w[:, k, :]) for w, a in parts(wo_h, wo_l, xh, xl) for k in range(KC)]
                    for j, (a, w) in enumerate(run):
                        last = T.matmul(att[u][t // 2][:, (t % 2) * DIM:(t % 2 + 1) * DIM], a, w,
                                        start=(j == 0), stop=(j == len(run) - 1))
                    if t % 2:
                        last.then_inc(att_ready, 1)

            pe.wait_ge(w_lo, 4)
            attention(0, 0)
            wait_down(NT - 1)
            for t in range(TT):
                down(1, t)
            pe.wait_ge(ms_read, NT - 1)
            squares_sum(NT - 1)
            pe.wait_ge(y_ready, 2 * NT)
            attention(1, 1)
            pe.wait_ge(ms_read, NT)
            pe.wait_ge(place, 1)
            T.matmul(m_wide[:, 0:E], ones[:, :], count[:, :], start=True, stop=True).then_inc(count_ready, 1)
            pe.wait_ge(o_ready, TT)
            attention(2, 0)
            pe.wait_ge(o_ready, 2 * TT)
            attention(3, 1, (0, 1))
            pe.wait_ge(code_ready, 1)
            T.transpose(m_wide, code, ident).then_inc(code_tr, 1)
            attention(3, 1, (2, 3))
            pe.wait_ge(code_sb, 1)
            T.transpose(m_wide, ab[:, 0:2, :].rearrange("p a c -> p (a c)"), ident).then_inc(a_tr, 1)
            for i in range(4, FIRST_ROW_TILE):
                pe.wait_ge(o_ready, TT * (i - 1))
                attention(i, i % 2)

            def gather(n, u, q):
                for r in range(RG):
                    j = RG * q + r
                    last = T.matmul(up[q % 2][:, r * HID:(r + 1) * HID],
                                    pair_hot_t[u][:, j * P:(j + 1) * P], a_hl[:, :], start=True, stop=True)
                last.then_inc(gathered, 1)

            def reduce(n, u, q):
                pe.wait_ge(row_silu, RPT * n + RG * (q + 1))
                for r in range(RG):
                    j = RG * q + r
                    last = T.matmul(up[2][:, 0:PAIRS], act_out[:, q % 2, r * HID:(r + 1) * HID],
                                    pair_w[u][:, j, :, :].rearrange("p g e -> p (g e)"),
                                    start=(j == 0), stop=(j == RPT - 1))
                last.then_inc(reduced, 1)

            def row_tile(n, u, last=False):
                i = FIRST_ROW_TILE + n
                banks = RPT // RG
                pe.wait_ge(o_ready, TT * (i - 1))
                attention(i, u, (0,))
                pe.wait_ge(pair_w_ready, n + 1)
                pe.wait_ge(s_added, n + 1)
                for q in range(banks):
                    reduce(n, u, q)
                    if q + 2 < banks:
                        gather(n, u, q + 2)
                    elif not last:
                        if q + 2 == banks:
                            pe.wait_ge(hot_ready, n + 2)
                        gather(n + 1, 1 - u, q + 2 - banks)
                    if q + 1 < TT:
                        attention(i, u, (q + 1,))

            pe.wait_ge(a_ready, 1)
            pe.wait_ge(hot_ready, 1)
            gather(0, 0, 0)
            gather(0, 0, 1)
            with pe.Fori(0, ROW_TILES // 2 - 1) as b:
                row_tile(2 * b, 0)
                row_tile(2 * b + 1, 1)
            row_tile(ROW_TILES - 2, 0)
            row_tile(ROW_TILES - 1, 1, last=True)
            pe.wait_ge(w2_in, 16)
            pe.wait_ge(h_pairs, 1)
            for g in range(E):
                last = T.matmul(misc[0:E, 0:DIM], s_sum[:, E * g:E * g + E], w2_sb[:, g, :],
                                start=(g == 0), stop=(g == E - 1))
            last.then_inc(routed, 1)


def constants():
    import numpy as np

    c = np.zeros((P, C_END), np.float32)
    p = np.arange(P)
    c[:, C_IDENT:C_IDENT + P] = np.eye(P)
    c[:, C_HEADS:C_HEADS + P] = (p[:, None] // 16 == p[None, :] // 16)
    for col, n in ((C_THR8, E), (C_THR4, GRP)):
        j, i = np.divmod(np.arange(n * n), n)
        c[:, col:col + n * n] = np.where(i < j, 0.0, LEAST)[None, :]
    j = np.arange(ROWT)
    c[:, C_POS:C_POS + ROWT] = 2 * P * (j // 2)[None, :] + 2 * p[:, None] + (j % 2)[None, :]
    c[:, C_IOTA:C_IOTA + E] = np.arange(E)
    c[:, C_PAIR] = p % PAIRS
    return c


def kernel(L0_attn_x, L0_attn_q, L0_attn_k, L0_attn_log_decay, L0_attn_norm_weight, L0_attn_o_w,
           L0_ffn_w_gate, L0_ffn_w1, L0_ffn_w2, L0_ffn_w3, L0_ffn_sw1, L0_ffn_sw2, L0_ffn_sw3,
           L0_ffn_expert_bias):
    import numpy as np
    import concourse.bacc as bacc
    from concourse.bass_utils import run_bass_kernel_spmd

    x = np.asarray(L0_attn_x)
    small = np.zeros((P, S_END), np.float32)

    def columns(v):
        return np.asarray(v).reshape(KC, P).T

    small[:, S_Q:S_Q + KC] = columns(L0_attn_q)
    small[:, S_K:S_K + KC] = columns(L0_attn_k)
    small[:, S_NW:S_NW + KC] = columns(L0_attn_norm_weight)
    small[:, S_LD:S_LD + KC] = columns(np.repeat(np.asarray(L0_attn_log_decay), DIM // 16))
    small[:, S_EB:S_END] = np.asarray(L0_ffn_expert_bias)[None, :]
    arrays = {
        "x": x.reshape(TOKENS, DIM),
        "small": small,
        "w_gate": np.asarray(L0_ffn_w_gate).T,
        "w_up": np.concatenate([np.asarray(L0_ffn_sw1).T, np.asarray(L0_ffn_sw3).T], axis=1),
        "w_down": np.asarray(L0_ffn_sw2).T,
        "w_o": np.asarray(L0_attn_o_w).T,
        "w1": np.asarray(L0_ffn_w1),
        "w2": np.asarray(L0_ffn_w2),
        "w3": np.asarray(L0_ffn_w3),
        "consts": constants(),
    }
    arrays = {n: np.ascontiguousarray(a) for n, a in arrays.items()}
    nc = bacc.Bacc("TRN2", target_bir_lowering=False, num_devices=1)
    args = [nc.dram_tensor(n, a.shape, mybir.dt.from_np(a.dtype), kind="ExternalInput").ap()
            for n, a in arrays.items()]
    out = nc.dram_tensor("out", (TOKENS, DIM), mybir.dt.float32, kind="ExternalOutput").ap()
    build(nc, *args, out)
    got = run_bass_kernel_spmd(nc, [arrays], core_ids=[0])
    return got.results[0]["out"].reshape(x.shape)
```

```python
import concourse.bass as bass
from concourse import mybir
from contextlib import ExitStack

P = 128
TOKENS, DIM = 8192, 256
KC = DIM // P
TILE = 512
HALF = TILE // 2
TT = TILE // P
NT = TOKENS // TILE
NB = NT // 2
NTT = TOKENS // P
E = 8
GRP = 4
HID = 128
TOPK = 2
ROWT = TOPK * NTT
FIRST_ROW_TILE = NT // 2
RPT = ROWT // (NT - FIRST_ROW_TILE)
ROW_TILES = NT - FIRST_ROW_TILE
RG = 4
PAIRS = E * E
QTR = DIM // 4
LN_EPS, RMS_EPS = 1e-5, 1e-6
CLOCK_PRODUCTS = 16
FAR = 1e38
LEAST = 1.1754944e-38

C_IDENT, C_HEADS, C_THR8, C_THR4, C_POS, C_IOTA, C_PAIR = 0, 128, 256, 320, 336, 464, 472
C_END = 473
S_Q, S_K, S_NW, S_LD, S_EB, S_END = 0, 2, 4, 6, 8, 16


def build(nc, x, small, w_gate, w_up, w_down, w_o, w1, w2, w3, consts, out):
    f32, f32r, bf16 = mybir.dt.float32, mybir.dt.float32r, mybir.dt.bfloat16
    ALU = mybir.AluOpType
    ACT = mybir.ActivationFunctionType
    AX = mybir.AxisListType
    V, G, A, T = nc.vector, nc.gpsimd, nc.scalar, nc.tensor

    x_v = x.rearrange("(n p) d -> p n d", p=P)
    out_v = out.rearrange("(n p) d -> p n d", p=P)
    codes_dram = nc.dram_tensor("row_codes", (ROWT, P), bf16, kind="Internal").ap()

    ctx = ExitStack()
    with ctx:
        def sb(name, shape, dt=f32):
            return ctx.enter_context(nc.sbuf_tensor(name, shape, dt))

        def bank(name):
            return ctx.enter_context(nc.psum_tensor(name, [P, 512], f32))

        def sem(name):
            return ctx.enter_context(nc.semaphore(name))

        x_sb = sb("x_sb", [P, NTT, DIM])
        e_sb = sb("e_sb", [P, KC, TOKENS])
        raw_up = e_sb[:, 0, 1024:2048].rearrange("p (k n) -> p k n", k=KC)
        raw_down = e_sb[:, 0, 2048:2560].rearrange("p (k n) -> p k n", k=KC)
        raw_o = e_sb[:, 0, 2560:3072].rearrange("p (k n) -> p k n", k=KC)
        raw_gate = e_sb[:, 0, 3072:3072 + KC * E].rearrange("p (k n) -> p k n", k=KC)
        w1_sb = e_sb[:, 0, 4096:6144].rearrange("p (k g h) -> p k g h", k=KC, g=E)
        w3_sb = e_sb[:, 1, 4096:6144].rearrange("p (k g h) -> p k g h", k=KC, g=E)
        w2_sb = e_sb[:, 0, 0:E * DIM].rearrange("p (g d) -> p g d", g=E)
        codes_bc = e_sb[:, 1, 0:RPT * P].bitcast(bf16).rearrange("p (u n) -> p u n", u=2)

        xn = sb("xn", [P, 2, TT, DIM])
        xh = sb("xh", [P, 2, KC, TILE], f32r)
        xl = sb("xl", [P, 2, KC, TILE], f32r)
        act_out = sb("act_out", [P, 2, TILE])
        hh = sb("hh", [P, 2, 2, TILE], f32r)
        hl = sb("hl", [P, 2, 2, TILE], f32r)
        sq = sb("sq", [P, KC, TILE])
        gate_rows = sq[0:2 * E, 1, :]
        ssq_rows = sq[:, 0, 0:P]
        ab_rows_sb = sq[:, 0, :]
        pair_hot_t = [t[:, :, :, :].rearrange("p a b n -> p (a b n)") for t in (hh, hl)]
        pair_w = [xn[:, u, :, :].rearrange("p a (b g e) -> p (a b) g e", g=E, e=E) for u in (0, 1)]

        wup_h = sb("wup_h", [P, KC, 512], f32r)
        wup_l = sb("wup_l", [P, KC, 512], f32r)
        wdn_h = sb("wdn_h", [P, KC, DIM], f32r)
        wdn_l = sb("wdn_l", [P, KC, DIM], f32r)
        wo_h = sb("wo_h", [P, KC, DIM], f32r)
        wo_l = sb("wo_l", [P, KC, DIM], f32r)
        wg_hl = sb("wg_hl", [P, KC, 2, E], f32r)

        cst = sb("cst", [P, C_END])
        ident = cst[:, C_IDENT:C_IDENT + P]
        heads = cst[:, C_HEADS:C_HEADS + P]
        thr8 = cst[:, C_THR8:C_THR8 + 64].rearrange("p (j i) -> p j i", j=E)
        thr4 = cst[:, C_THR4:C_THR4 + 16].rearrange("p (j i) -> p j i", j=GRP)
        pos = cst[:, C_POS:C_POS + ROWT]
        iota = cst[:, C_IOTA:C_IOTA + E]
        pair_no = cst[:, C_PAIR:C_PAIR + 1]
        par = sb("par", [P, S_END])
        ones = sb("ones", [P, P])
        lam = sb("lam", [P, KC])
        qk = sb("qk", [P, KC])
        c_col = sb("c_col", [P, KC])
        o_scale = sb("o_scale", [P, KC])

        stats = sb("stats", [P, TT, 6])
        mean_var = sb("mean_var", [P, TT, 2])
        var_eps = sb("var_eps", [P, 2, TT])
        neg_mean = sb("neg_mean", [P, 2, TT])
        rstd = sb("rstd", [P, 2, TT])
        shift = sb("shift", [P, 2, TT])
        power = sb("power", [P, E])
        ms = sb("ms", [P, NTT])
        rms = sb("rms", [P, NTT])

        logit = sb("logit", [P, E, E])
        top = sb("top", [P, E])
        prob = sb("prob", [P, E, E])
        total = sb("total", [P, E])
        score = sb("score", [P, E, E])
        gscore = sb("gscore", [P, E, GRP])
        grank = sb("grank", [P, E, GRP])
        diff = sb("diff", [P, E, E, E])
        flat_diff = diff[:, :, :, :].rearrange("p t j i -> p (t j i)")
        gdiff = flat_diff[:, 0:E * GRP * GRP].rearrange("p (t j i) -> p t j i", t=E, j=GRP)
        scaled_pick = flat_diff[:, 0:2 * E * E].rearrange("p (r e) -> p r e", e=E)
        x32 = flat_diff[:, 0:KC * 32].rearrange("p (k n) -> p k n", k=KC)
        rank = sb("rank", [P, E, E])
        pick = sb("pick", [P, ROWT, E], bf16)
        pick_w = sb("pick_w", [P, ROWT, E])
        row_w = sb("row_w", [P, ROWT])
        row_e = sb("row_e", [P, ROWT])

        ab = sb("ab", [P, 3, PAIRS])
        a_hl = sb("a_hl", [P, HID], f32r)
        group_hot = sq[:, 0, :].bitcast(bf16).rearrange("p (j g) -> p j g", g=E)
        row_g = sq[:, 1, 0:ROWT]
        code = sq[:, 1, 128:128 + ROWT]
        a_t = sq[:, 1, 256:256 + HID]
        sums_b = sq[:, 1, 384:384 + P]
        count = sb("count", [P, E])
        ends = sb("ends", [P, E])
        past = flat_diff.bitcast(bf16).rearrange("p (j g) -> p j g", g=E)
        code_t = sb("code_t", [P, P], bf16)
        row_w_now = sb("row_w_now", [P, 2, RPT])
        warm = sb("warm", [P, 1])
        h_sum = sb("h_sum", [P, PAIRS])

        tp = [bank("tp0"), bank("tp1")]
        up = [bank("up0"), bank("up1"), bank("up2")]
        dn = [bank("dn0"), bank("dn1")]
        misc = bank("misc")
        m_gate = misc[:, 0:2 * E * TT]
        m_ssq = misc[:, P:2 * P]
        m_ssq_rows = misc[:, 2 * P:3 * P]
        ab_rows, ab_t = dn[0], dn[1][:, :].rearrange("p (g c e) -> p c g e", g=4, c=4)
        m_wide = misc[:, 384:512]
        att = [tp, dn]

        x_in = [sem("x_in0"), sem("x_in1")]
        small_in, bias_in, cst_in = sem("small_in"), sem("bias_in"), sem("cst_in")
        x_first = sem("x_first")
        up_in, gate_in, w13_in = sem("up_in"), sem("gate_in"), sem("w13_in")
        down_in, o_in = sem("down_in"), sem("o_in")
        w2_in = sem("w2_in")
        codes_out = sem("codes_out")
        codes_in = [sem("codes_in0"), sem("codes_in1")]
        stored = sem("stored")
        ones_set = sem("ones_set")
        setup = sem("setup")
        decay_exp, power_set, qk_sum = sem("decay_exp"), sem("power_set"), sem("qk_sum")
        params = sem("params")
        o_scaled = sem("o_scaled")
        w_hi, w_lo = sem("w_hi"), sem("w_lo")
        stat_step = sem("stat_step")
        ln_stats = sem("ln_stats")
        rstd_step, rstd_ready = sem("rstd_step"), sem("rstd_ready")
        xn_ready = sem("xn_ready")
        tp_ready = sem("tp_ready")
        xh_ready, xl_ready = sem("xh_ready"), sem("xl_ready")
        e_ready = sem("e_ready")
        up_ready = sem("up_ready")
        silu_ready, h_ready = sem("silu_ready"), sem("h_ready")
        hh_ready, hl_ready = sem("hh_ready"), sem("hl_ready")
        sq_ready, sq_added = sem("sq_ready"), sem("sq_added")
        gate_ready, gate_sb = sem("gate_ready"), sem("gate_sb")
        ssq_ready, ssq_sb = sem("ssq_ready"), sem("ssq_sb")
        misc_ready = sem("misc_ready")
        ms_read, logit_read = sem("ms_read"), sem("logit_read")
        dn_ready, y_ready = sem("dn_ready"), sem("y_ready")
        route = sem("route")
        exp_ready = sem("exp_ready")
        rms_ready = sem("rms_ready")
        x32_ready, ab_read = sem("x32_ready"), sem("ab_read")
        ab_ready, ab_sb = sem("ab_ready"), sem("ab_sb")
        eh_ready, el_ready = sem("eh_ready"), sem("el_ready")
        att_ready = sem("att_ready")
        o_ready = sem("o_ready")
        place = sem("place")
        count_ready, code_ready, code_tr = sem("count_ready"), sem("code_ready"), sem("code_tr")
        a_tr, a_ready = sem("a_tr"), sem("a_ready")
        code_sb = sem("code_sb")
        hot_ready, pair_w_ready = sem("hot_ready"), sem("pair_w_ready")
        roww_ready = sem("roww_ready")
        gathered = sem("gathered")
        row_silu = sem("row_silu")
        reduced = sem("reduced")
        zeros_set = sem("zeros_set")
        sums_sb, sums_tr = sem("sums_sb"), sem("sums_tr")
        h_pairs, routed, first8_ready = sem("h_pairs"), sem("routed"), sem("first8_ready")

        ROUTE_STEPS = 21

        def token_tile(i, t):
            return x_sb[:, bass.ds(TT * i + t, 1), :].rearrange("p a d -> p (a d)")

        block = ctx.enter_context(nc.Block())

        @block.sync
        def _(sp):
            sp.dma_start(x_sb[:, 0:2, :], x_v[:, 0:2, :]).then_inc(x_first, 16)
            sp.dma_start(x_sb[:, 2:TT, :], x_v[:, 2:TT, :]).then_inc(x_in[0], 16)
            sp.dma_start(par[:, 0:S_EB], small[:, 0:S_EB]).then_inc(small_in, 16)
            sp.dma_start(x_sb[:, TT:2 * TT, :], x_v[:, TT:2 * TT, :]).then_inc(x_in[1], 16)
            for k in range(KC):
                sp.dma_start(w1_sb[:, k, :, :], w1[:, k * P:(k + 1) * P, :].rearrange("g p h -> p g h"))\
                    .then_inc(w13_in, 16)
                sp.dma_start(w3_sb[:, k, :, :], w3[:, k * P:(k + 1) * P, :].rearrange("g p h -> p g h"))\
                    .then_inc(w13_in, 16)
            sp.dma_start(raw_down, w_down.rearrange("(k p) n -> p k n", p=P)).then_inc(down_in, 16)
            sp.dma_start(raw_o, w_o.rearrange("(k p) n -> p k n", p=P)).then_inc(o_in, 16)
            sp.dma_start(par[:, S_EB:S_END], small[0:1, S_EB:S_END].to_broadcast([P, E])).then_inc(bias_in, 16)
            with sp.Fori(1, NB) as b:
                for u in range(2):
                    i = 2 * b + u
                    sp.wait_ge(x_in[u], 16 * b)
                    sp.dma_start(x_sb[:, bass.ds(TT * i, TT), :],
                                 x_v[:, bass.ds(TT * i, TT), :]).then_inc(x_in[u], 16)

            sp.wait_ge(o_ready, TT)
            sp.dma_start(out_v[E:P, 0, :], x_sb[E:P, 0, :]).then_inc(stored, 16)
            sp.dma_start(out_v[:, 1:TT, :], x_sb[:, 1:TT, :]).then_inc(stored, 16)

            def store(i):
                sp.wait_ge(o_ready, TT * i + TT)
                sp.dma_start(out_v[:, bass.ds(TT * i, TT), :],
                             x_sb[:, bass.ds(TT * i, TT), :]).then_inc(stored, 16)

            store(1)
            store(2)
            sp.wait_ge(eh_ready, 2 * 4)
            sp.wait_ge(el_ready, 2 * 4)
            sp.wait_ge(code_sb, 1)
            sp.dma_start(codes_dram, code_t[:, :]).then_inc(codes_out, 16)
            sp.wait_ge(codes_out, 16)
            for u in range(2):
                sp.dma_start(codes_bc[:, u, :], codes_dram[RPT * u:RPT * (u + 1), :]
                             .rearrange("(o j) n -> o (j n)", o=1).to_broadcast([P, RPT * P]))\
                    .then_inc(codes_in[u], 16)
            with sp.Fori(3, FIRST_ROW_TILE) as i:
                store(i)
            sp.dma_start(w2_sb, w2.rearrange("g h d -> h g d")).then_inc(w2_in, 16)
            with sp.Fori(0, (NT - FIRST_ROW_TILE) // 2 - 1) as b:
                for u in range(2):
                    i = FIRST_ROW_TILE + 2 * b + u
                    sp.wait_ge(hot_ready, 2 * b + u + 1)
                    sp.dma_start(codes_bc[:, u, :],
                                 codes_dram[bass.ds(RPT * (2 * b + u + 2), RPT), :]
                                 .rearrange("(o j) n -> o (j n)", o=1).to_broadcast([P, RPT * P]))\
                        .then_inc(codes_in[u], 16)
                    store(i)
            store(NT - 2)
            for t in range(0, TT, 2):
                sp.wait_ge(o_ready, TT * (NT - 1) + t + 2)
                sp.dma_start(out_v[:, TT * (NT - 1) + t:TT * (NT - 1) + t + 2, :],
                             x_sb[:, TT * (NT - 1) + t:TT * (NT - 1) + t + 2, :]).then_inc(stored, 16)
            sp.wait_ge(first8_ready, 4)
            sp.dma_start(out[0:E, :], x_sb[0:E, 0, :]).then_inc(stored, 16)
            sp.wait_ge(stored, 16 * (NT + 3))

        @block.gpsimd
        def _(pool):
            G.memset(power[:, :], -0.5).then_inc(power_set, 1)
            pool.wait_ge(power_set, 1)

            def token_scale(i, u):
                pool.wait_ge(ln_stats, 2 * i + 2)
                if not (isinstance(i, int) and i < 2):
                    pool.wait_ge(xn_ready, TT * (i - 1))
                G.tensor_tensor(rstd[:, u, :], var_eps[:, u, :], power[:, 0:TT], ALU.pow).then_inc(rstd_step, 1)
                pool.wait_ge(rstd_step, i + 1)
                G.tensor_tensor(shift[:, u, :], neg_mean[:, u, :], rstd[:, u, :], ALU.mult).then_inc(rstd_ready, 1)

            def sum_squares(i):
                pool.wait_ge(sq_ready, 2 * i + 2)
                G.tensor_tensor(sq[:, 0, :], sq[:, 0, :], sq[:, 1, :], ALU.add).then_inc(sq_added, 1)

            def h_lo(i, u, m):
                pool.wait_ge(hh_ready, 2 * i + m + 1)
                G.tensor_tensor(hl[:, u, m, :], act_out[:, m, :], hh[:, u, m, :].bitcast(f32),
                                ALU.subtract).then_inc(hl_ready, 1)

            def rms_factors(b):
                pool.wait_ge(ms_read, 2 * b + 2)
                at = bass.ds(E * b, E)
                G.tensor_tensor(rms[:, at], ms[:, at], power[:, :], ALU.pow).then_inc(rms_ready, 1)

            def weight_lo(lo, hi, raw, n):
                pool.wait_ge(w_hi, n)
                G.tensor_tensor(lo, raw, hi.bitcast(f32), ALU.subtract).then_inc(w_lo, 1)

            def batch(b, first=False, last=False):
                for u in range(2):
                    i = 2 * b + u
                    if not (first and u == 0):
                        sum_squares(i - 1)
                    if not last:
                        token_scale(i + 2, u)
                    h_lo(i, u, 0)
                    if u == 1 and not first:
                        rms_factors(b - 1)
                    if last and u == 1:
                        e_lo(0, 0)
                    if first and u == 0:
                        weight_lo(wdn_l[:, :, :], wdn_h[:, :, :], raw_down, 3)
                    elif first:
                        weight_lo(wo_l[:, :, :], wo_h[:, :, :], raw_o, 4)
                    h_lo(i, u, 1)

            def e_lo(i, u):
                for h in range(2):
                    half = slice(h * HALF, (h + 1) * HALF)
                    pool.wait_ge(eh_ready, 2 * i + h + 1)
                    G.tensor_tensor(xl[:, u, :, half], e_sb[:, :, bass.ds(TILE * i + h * HALF, HALF)],
                                    xh[:, u, :, half].bitcast(f32), ALU.subtract).then_inc(el_ready, 1)

            token_scale(0, 0)
            weight_lo(wup_l[:, :, :], wup_h[:, :, :], raw_up, 1)
            token_scale(1, 1)
            weight_lo(wg_hl[:, :, 1, :], wg_hl[:, :, 0, :], raw_gate, 2)
            batch(0, first=True)
            with pool.Fori(1, NB - 1) as b:
                batch(b)
            batch(NB - 1, last=True)
            e_lo(1, 1)
            sum_squares(NT - 1)
            e_lo(2, 0)
            e_lo(3, 1)
            with pool.Fori(2, FIRST_ROW_TILE // 2 + 1) as b:
                for u in range(2):
                    e_lo(2 * b + u, u)
            rms_factors(NB - 1)
            with pool.Fori(FIRST_ROW_TILE // 2 + 1, NB) as b:
                for u in range(2):
                    e_lo(2 * b + u, u)

        @block.scalar
        def _(act):
            act.dma_start(cst[:, :], consts).then_inc(cst_in, 16)
            act.dma_start(raw_up, w_up.rearrange("(k p) n -> p k n", p=P)).then_inc(up_in, 16)
            act.dma_start(raw_gate, w_gate.rearrange("(k p) n -> p k n", p=P)).then_inc(gate_in, 16)
            act.wait_ge(small_in, 16)
            A.activation(lam[:, :], par[:, S_LD:S_LD + KC], ACT.Exp, scale=-1.0).then_inc(decay_exp, 1)

            def normalize(i, u):
                act.wait_ge(rstd_ready, i + 1)
                if not (isinstance(i, int) and i < 2):
                    act.wait_ge(tp_ready, 2 * i - 2)
                for t in range(TT):
                    A.activation(xn[:, u, t, :], token_tile(i, t), ACT.Identity, bias=shift[:, u, t:t + 1],
                                 scale=rstd[:, u, t:t + 1]).then_inc(xn_ready, 1)

            def x_hi(i, u):
                for k in range(KC):
                    act.wait_ge(tp_ready, 2 * i + k + 1)
                    A.activation(xh[:, u, k, :], tp[k][:, :], ACT.Copy).then_inc(xh_ready, 1)

            def silu(i, m, first=False):
                act.wait_ge(up_ready, 4 * i + 2 * m + 1)
                if not first:
                    act.wait_ge(hl_ready, 2 * i + m - 1)
                A.activation(act_out[:, m, :], up[2 * m][:, :], ACT.Silu).then_inc(silu_ready, 1)

            def h_hi(i, u, m, first=False):
                act.wait_ge(h_ready, 2 * i + m + 1)
                if not first:
                    act.wait_ge(dn_ready, 2 * i - 2)
                A.activation(hh[:, u, m, :], act_out[:, m, :], ACT.Copy).then_inc(hh_ready, 1)

            def gate_copy(i):
                act.wait_ge(gate_ready, i + 1)
                if not (isinstance(i, int) and i == 0):
                    act.wait_ge(sq_added, i)
                A.activation(gate_rows, up[1][0:2 * E, :], ACT.Copy).then_inc(gate_sb, 1)

            def ssq_copy(i):
                act.wait_ge(ssq_ready, i + 1)
                A.activation(ssq_rows, m_ssq_rows, ACT.Copy).then_inc(ssq_sb, 1)

            def squares(i):
                act.wait_ge(e_ready, 2 * i + 2)
                act.wait_ge(misc_ready, i + 1)
                for k in range(KC):
                    A.activation(sq[:, k, :], e_sb[:, k, bass.ds(TILE * i, TILE)], ACT.Square,
                                 scale=c_col[:, k:k + 1]).then_inc(sq_ready, 1)

            def router_exp(b):
                act.wait_ge(route, ROUTE_STEPS * b + 2)
                A.activation(prob[:, :, :], prob[:, :, :], ACT.Exp).then_inc(exp_ready, 1)

            def weight_hi(hi, raw):
                A.activation(hi, raw, ACT.Copy).then_inc(w_hi, 1)

            def down_weights():
                act.wait_ge(down_in, 16)
                weight_hi(wdn_h[:, :, :], raw_down)

            def output_weights():
                act.wait_ge(o_in, 16)
                act.wait_ge(params, 1)
                for k in range(KC):
                    A.activation(raw_o[:, k, :], raw_o[:, k, :], ACT.Copy, scale=o_scale[:, k:k + 1])\
                        .then_inc(o_scaled, 1)
                act.wait_ge(o_scaled, KC)
                weight_hi(wo_h[:, :, :], raw_o)

            def batch(b, first=False, last=False):
                for u in range(2):
                    i = 2 * b + u
                    silu(i, 0, first and u == 0)
                    if not (first and u == 0):
                        squares(i - 1)
                    if last and u == 1:
                        act.wait_ge(misc_ready, NT - 1)
                        e_hi_half(0, 0, 0)
                        e_hi_half(0, 0, 1)
                    else:
                        x_hi(i + 1, 1 - u)
                    if u == 0 and not first:
                        router_exp(b - 1)
                    else:
                        h_hi(i, u, 0, first)
                    silu(i, 1, first and u == 0)
                    if u == 0 and not first:
                        h_hi(i, u, 0)
                    if first and u == 0:
                        act.wait_ge(ab_ready, 1)
                        A.activation(ab_rows_sb, ab_rows[:, :], ACT.Copy).then_inc(ab_sb, 1)
                    if first:
                        (down_weights, output_weights)[u]()
                    gate_copy(i)
                    if not (first and u == 0):
                        ssq_copy(i - 1)
                    h_hi(i, u, 1, first)
                    if not last:
                        normalize(i + 2, u)
                    elif u == 1:
                        router_exp(b)

            def e_hi_half(i, u, h):
                A.activation(xh[:, u, :, h * HALF:(h + 1) * HALF], e_sb[:, :, bass.ds(TILE * i + h * HALF, HALF)],
                             ACT.Copy).then_inc(eh_ready, 1)

            def e_hi(i, u, h):
                act.wait_ge(att_ready, 2 * i + h - 3)
                e_hi_half(i, u, h)

            act.wait_ge(up_in, 16)
            weight_hi(wup_h[:, :, :], raw_up)
            normalize(0, 0)
            x_hi(0, 0)
            act.wait_ge(gate_in, 16)
            weight_hi(wg_hl[:, :, 0, :], raw_gate)
            normalize(1, 1)
            batch(0, first=True)
            with act.Fori(1, NB - 1) as b:
                batch(b)
            batch(NB - 1, last=True)
            act.wait_ge(misc_ready, NT)
            e_hi_half(1, 1, 0)
            e_hi_half(1, 1, 1)
            squares(NT - 1)
            for h in range(2):
                e_hi(2, 0, h)
            ssq_copy(NT - 1)
            for h in range(2):
                e_hi(3, 1, h)
            with act.Fori(2, FIRST_ROW_TILE // 2) as b:
                for u in range(2):
                    for h in range(2):
                        e_hi(2 * b + u, u, h)

            e_hi(FIRST_ROW_TILE, 0, 0)
            e_hi(FIRST_ROW_TILE, 0, 1)
            A.activation(warm[:, :], ones[:, 0:1], ACT.Silu)

            def rows(n, u, last=False):
                act.wait_ge(roww_ready, n + 1)
                for q in range(RPT // RG):
                    act.wait_ge(gathered, (RPT // RG) * n + q + 1)
                    if q >= 2:
                        act.wait_ge(reduced, (RPT // RG) * n + q - 1)
                    for r in range(RG):
                        j = RG * q + r
                        A.activation(act_out[:, q % 2, r * HID:(r + 1) * HID],
                                     up[q % 2][:, r * HID:(r + 1) * HID], ACT.Silu,
                                     scale=row_w_now[:, u, j:j + 1]).then_inc(row_silu, 1)
                    if q < 2 and not last:
                        e_hi(FIRST_ROW_TILE + n + 1, 1 - u, q)

            with act.Fori(0, ROW_TILES // 2 - 1) as b:
                rows(2 * b, 0)
                rows(2 * b + 1, 1)
            rows(ROW_TILES - 2, 0)
            rows(ROW_TILES - 1, 1, last=True)

        @block.vector
        def _(dve):
            at_setup = 0

            def done(ins):
                nonlocal at_setup
                at_setup += 1
                ins.then_inc(setup, 1)
                dve.wait_ge(setup, at_setup)

            def bn(i, tiles=range(TT)):
                for t in tiles:
                    V.bn_stats(stats[:, t, :], token_tile(i, t)).then_inc(stat_step, 1)

            def wait_bn(i):
                dve.wait_ge(stat_step, 2 * TT * i + TT)

            def aggregate(i):
                for t in range(TT):
                    V.bn_aggr(mean_var[:, t, :], stats[:, t, :]).then_inc(stat_step, 1)

            def finish_stats(i, u):
                dve.wait_ge(stat_step, 2 * TT * i + 2 * TT)
                if not (isinstance(i, int) and i < 2):
                    dve.wait_ge(rstd_ready, i - 1)
                V.tensor_scalar(var_eps[:, u, :], mean_var[:, :, 1], LN_EPS, None, ALU.add).then_inc(ln_stats, 1)
                V.tensor_scalar(neg_mean[:, u, :], mean_var[:, :, 0], -1.0, None, ALU.mult).then_inc(ln_stats, 1)

            def x_lo(i, u, k):
                dve.wait_ge(xh_ready, 2 * i + k + 1)
                V.tensor_tensor(xl[:, u, k, :], tp[k][:, :], xh[:, u, k, :].bitcast(f32),
                                ALU.subtract).then_inc(xl_ready, 1)

            def scan(i, u, k):
                if u:
                    dve.wait_ge(e_ready, 2 * i + k - 1)
                start = e_sb[:, k, bass.ds(TILE * i - 1, 1)] if u else 0.0
                V.tensor_tensor_scan(e_sb[:, k, bass.ds(TILE * i, TILE)], lam[:, k:k + 1].to_broadcast([P, TILE]),
                                     tp[k][:, :], start, ALU.mult, ALU.add).then_inc(e_ready, 1)

            def gate_mul(i, m):
                dve.wait_ge(silu_ready, 2 * i + m + 1)
                dve.wait_ge(up_ready, 4 * i + 2 * m + 2)
                V.tensor_tensor(act_out[:, m, :], act_out[:, m, :], up[1 - m][:, :], ALU.mult).then_inc(h_ready, 1)

            def add_shared(i, a):
                dve.wait_ge(dn_ready, 2 * i + a + 1)
                at = x_sb[:, bass.ds(TT * i + 2 * a, 2), :]
                V.tensor_tensor(at, dn[a][:, :].rearrange("p (t d) -> p t d", t=2), at, ALU.add).then_inc(y_ready, 1)

            def read_mean_square(i):
                dve.wait_ge(misc_ready, i + 2)
                V.tensor_scalar(ms[:, bass.ds(TT * i, TT)], m_ssq[:, 0:P:P // TT], 1.0 / DIM, RMS_EPS, ALU.mult, ALU.add)\
                    .then_inc(ms_read, 1)

            def read_logits(i, u):
                dve.wait_ge(misc_ready, i + 1)
                V.tensor_reduce(logit[:, TT * u:TT * u + TT, :],
                                m_gate.rearrange("p (t h e) -> p t e h", h=2, e=E), AX.X,
                                ALU.add).then_inc(logit_read, 1)

            def after(b, n):
                dve.wait_ge(route, ROUTE_STEPS * b + n)

            def over_experts(t):
                return t[:, :].unsqueeze(2).to_broadcast([P, E, E])

            def route_max(b):
                dve.wait_ge(logit_read, 2 * b + 2)
                V.tensor_reduce(top[:, :], logit[:, :, :], AX.X, ALU.max).then_inc(route, 1)

            def route_shift(b):
                after(b, 1)
                V.tensor_tensor(prob[:, :, :], logit[:, :, :], over_experts(top), ALU.subtract).then_inc(route, 1)

            def route_total(b):
                dve.wait_ge(exp_ready, b + 1)
                V.tensor_reduce(total[:, :], prob[:, :, :], AX.X, ALU.add).then_inc(route, 1)

            def route_invert(b):
                after(b, 3)
                V.reciprocal(total[:, :], total[:, :]).then_inc(route, 1)

            def route_prob(b):
                after(b, 4)
                V.tensor_tensor(prob[:, :, :], prob[:, :, :], over_experts(total), ALU.mult).then_inc(route, 1)

            def route_score(b):
                after(b, 5)
                V.tensor_tensor(score[:, :, :], prob[:, :, :],
                                par[:, S_EB:S_END].unsqueeze(1).to_broadcast([P, E, E]), ALU.add).then_inc(route, 1)

            score_pairs = score[:, :, :].rearrange("p t (g h) -> p t g h", h=2)

            def route_group_score(b):
                after(b, 6)
                V.tensor_tensor(gscore[:, :, :], score_pairs[:, :, :, 0], score_pairs[:, :, :, 1],
                                ALU.add).then_inc(route, 1)

            def route_group_diff(b):
                after(b, 7)
                V.tensor_tensor(gdiff, gscore[:, :, :].unsqueeze(2).to_broadcast([P, E, GRP, GRP]),
                                gscore[:, :, :].unsqueeze(3).to_broadcast([P, E, GRP, GRP]),
                                ALU.subtract).then_inc(route, 1)

            def route_group_before(b):
                after(b, 8)
                V.tensor_tensor(gdiff, gdiff, thr4.unsqueeze(1).to_broadcast([P, E, GRP, GRP]),
                                ALU.is_ge).then_inc(route, 1)

            def route_group_rank(b):
                after(b, 9)
                V.tensor_reduce(grank[:, :, :], gdiff, AX.X, ALU.add).then_inc(route, 1)

            def route_group_penalty(b):
                after(b, 10)
                V.tensor_scalar(grank[:, :, :], grank[:, :, :], 1.5, -FAR, ALU.is_gt, ALU.mult).then_inc(route, 1)

            def route_mask(b):
                after(b, 11)
                V.tensor_tensor(score_pairs, score_pairs,
                                grank[:, :, :].unsqueeze(3).to_broadcast([P, E, GRP, 2]), ALU.add).then_inc(route, 1)

            def route_diff(b):
                after(b, 12)
                V.tensor_tensor(diff[:, :, :, :], score[:, :, :].unsqueeze(2).to_broadcast([P, E, E, E]),
                                score[:, :, :].unsqueeze(3).to_broadcast([P, E, E, E]), ALU.subtract).then_inc(route, 1)

            def route_before(b):
                after(b, 13)
                V.tensor_tensor(diff[:, :, :, :], diff[:, :, :, :],
                                thr8.unsqueeze(1).to_broadcast([P, E, E, E]), ALU.is_ge).then_inc(route, 1)

            def route_rank(b):
                after(b, 14)
                V.tensor_reduce(rank[:, :, :], diff[:, :, :, :], AX.X, ALU.add).then_inc(route, 1)

            def rows_of(b):
                return bass.ds(2 * E * b, 2 * E)

            def choices(t, b):
                return t[:, rows_of(b), :].rearrange("p (t k) e -> p t k e", k=TOPK)

            def route_pick(b):
                after(b, 15)
                for k in range(TOPK):
                    V.tensor_scalar(choices(pick, b)[:, :, k, :], rank[:, :, :], float(k), None,
                                    ALU.is_equal).then_inc(route, 1)

            def route_pick_weight(b):
                after(b, 17)
                V.tensor_tensor(choices(pick_w, b), choices(pick, b),
                                prob[:, :, :].unsqueeze(2).to_broadcast([P, E, TOPK, E]), ALU.mult).then_inc(route, 1)

            def route_pick_number(b):
                after(b, 17)
                V.tensor_tensor(scaled_pick, pick[:, rows_of(b), :],
                                iota.unsqueeze(1).to_broadcast([P, 2 * E, E]), ALU.mult).then_inc(route, 1)

            def route_row_weight(b):
                after(b, 18)
                V.tensor_reduce(row_w[:, rows_of(b)], pick_w[:, rows_of(b), :], AX.X, ALU.add).then_inc(route, 1)

            def route_row_expert(b):
                after(b, 19)
                V.tensor_reduce(row_e[:, rows_of(b)], scaled_pick, AX.X, ALU.add).then_inc(route, 1)

            V.memset(ones[:, :], 1.0).then_inc(ones_set, 1)
            V.memset(h_sum[:, :], 0.0).then_inc(zeros_set, 1)
            dve.wait_ge(x_first, 16)
            bn(0, (0, 1))
            dve.wait_ge(x_in[0], 16)
            bn(0, (2, 3))
            wait_bn(0)
            aggregate(0)
            finish_stats(0, 0)
            dve.wait_ge(small_in, 16)
            done(V.tensor_tensor(qk[:, :], par[:, S_Q:S_Q + KC], par[:, S_K:S_K + KC], ALU.mult))
            dve.wait_ge(decay_exp, 1)
            done(V.tensor_scalar(lam[:, :], lam[:, :], 1.0, None, ALU.add))
            done(V.reciprocal(lam[:, :], lam[:, :]))
            dve.wait_ge(x_in[1], 16)
            bn(1)
            wait_bn(1)
            aggregate(1)
            finish_stats(1, 1)
            for k in range(KC):
                x_lo(0, 0, k)
            for k in range(KC):
                V.tensor_copy(x32[:, k, :], tp[k][:, 0:32]).then_inc(x32_ready, 1)
            for k in range(KC):
                scan(0, 0, k)
            dve.wait_ge(qk_sum, 1)
            done(V.tensor_copy(c_col[:, :], m_wide[:, 0:KC]))
            V.tensor_tensor(o_scale[:, :], c_col[:, :], par[:, S_NW:S_NW + KC], ALU.mult).then_inc(params, 1)
            dve.wait_ge(bias_in, 16)

            def read_tables():
                dve.wait_ge(misc_ready, 1)
                for slot, a in enumerate((0, 0, 1)):
                    V.tensor_copy(ab[:, slot, :].rearrange("p (c g e) -> p c g e", c=2, g=4),
                                  ab_t[:, 2 * a:2 * a + 2, :, 0:E]).then_inc(ab_read, 1)

            def batch(b, first=False, last=False):
                r = b - 1
                i = 2 * b
                if not first:
                    read_mean_square(i - 2)
                    read_logits(i - 1, 1)
                    add_shared(i - 2, 0)
                    route_max(r)
                    add_shared(i - 2, 1)
                    route_shift(r)
                gate_mul(i, 0)
                if not last:
                    dve.wait_ge(x_in[0], 16 * (b + 2))
                    bn(i + 2)
                    wait_bn(i + 2)
                x_lo(i + 1, 1, 0)
                if not last:
                    aggregate(i + 2)
                    finish_stats(i + 2, 0)
                gate_mul(i, 1)
                x_lo(i + 1, 1, 1)
                scan(i + 1, 1, 0)
                scan(i + 1, 1, 1)

                if first:
                    read_tables()

                i = 2 * b + 1
                if not first:
                    read_mean_square(i - 2)
                read_logits(i - 1, 0)
                if not first:
                    add_shared(i - 2, 0)
                    route_total(r)
                    add_shared(i - 2, 1)
                    route_invert(r)
                    route_prob(r)
                gate_mul(i, 0)
                if not last:
                    dve.wait_ge(x_in[1], 16 * (b + 2))
                    bn(i + 2)
                    wait_bn(i + 2)
                if not first:
                    route_score(r)
                if not last:
                    aggregate(i + 2)
                if not first:
                    route_group_score(r)
                if not last:
                    finish_stats(i + 2, 1)
                    x_lo(i + 1, 0, 0)
                if not first:
                    route_group_diff(r)
                if not last:
                    x_lo(i + 1, 0, 1)
                if not first:
                    route_group_before(r)
                if not last:
                    scan(i + 1, 0, 0)
                if not first:
                    route_group_rank(r)
                if not last:
                    scan(i + 1, 0, 1)
                if not first:
                    route_group_penalty(r)
                if not last:
                    gate_mul(i, 1)
                if not first:
                    route_mask(r)
                    route_diff(r)
                    route_before(r)
                    route_rank(r)
                    route_pick(r)
                    route_pick_weight(r)
                    route_pick_number(r)
                    route_row_weight(r)
                    route_row_expert(r)
                if last:
                    gate_mul(i, 1)

            batch(0, first=True)
            with dve.Fori(1, NB - 1) as b:
                batch(b)
            batch(NB - 1, last=True)
            def add_attention(i, u, tiles=range(TT)):
                for t in tiles:
                    if t % 2 == 0:
                        dve.wait_ge(att_ready, 2 * i + t // 2 + 1)
                    at = token_tile(i, t)
                    V.scalar_tensor_tensor(at, att[u][t // 2][:, (t % 2) * DIM:(t % 2 + 1) * DIM],
                                           rms[:, bass.ds(TT * i + t, 1)], at, ALU.mult, ALU.add).then_inc(o_ready, 1)

            last = NB - 1
            read_logits(NT - 1, 1)
            route_max(last)
            route_shift(last)
            add_shared(NT - 2, 0)
            add_shared(NT - 2, 1)
            route_total(last)
            read_mean_square(NT - 2)
            route_invert(last)
            route_prob(last)
            route_score(last)
            route_group_score(last)
            route_group_diff(last)
            route_group_before(last)
            route_group_rank(last)
            add_shared(NT - 1, 0)
            route_group_penalty(last)
            route_mask(last)
            add_shared(NT - 1, 1)
            dve.wait_ge(rms_ready, NB - 1)
            add_attention(0, 0, (0,))
            route_diff(last)
            route_before(last)
            add_attention(0, 0, (1,))
            route_rank(last)
            add_attention(0, 0, (2,))
            route_pick(last)
            add_attention(0, 0, (3,))
            dve.wait_ge(route, ROUTE_STEPS * NB - 4)
            V.tensor_reduce(count[:, :], pick[:, :, :].rearrange("p j e -> p e j"), AX.X, ALU.add).then_inc(place, 1)
            read_mean_square(NT - 1)
            route_pick_weight(last)
            route_pick_number(last)
            add_attention(1, 1, (0,))
            route_row_weight(last)
            add_attention(1, 1, (1,))
            route_row_expert(last)
            dve.wait_ge(count_ready, 1)
            V.tensor_tensor_scan(ends[:, :], ones[:, 0:E], m_wide[:, 0:E], 0.0, ALU.mult, ALU.add).then_inc(place, 1)
            add_attention(1, 1, (2, 3))
            dve.wait_ge(place, 2)
            V.tensor_tensor(past, pos.unsqueeze(2).to_broadcast([P, ROWT, E]),
                            ends[:, :].unsqueeze(1).to_broadcast([P, ROWT, E]), ALU.is_ge).then_inc(place, 1)
            add_attention(2, 0, (0, 1))
            dve.wait_ge(place, 3)
            V.tensor_reduce(row_g, past, AX.X, ALU.add).then_inc(place, 1)
            dve.wait_ge(place, 4)
            V.scalar_tensor_tensor(code, row_g, float(E), row_e[:, :], ALU.mult, ALU.add)\
                .then_inc(code_ready, 1)
            add_attention(2, 0, (2, 3))
            add_attention(3, 1, (0,))
            dve.wait_ge(code_tr, 1)
            V.tensor_copy(code_t[:, :], m_wide).then_inc(code_sb, 1)
            add_attention(3, 1, (1, 2, 3))
            V.tensor_tensor(group_hot, row_g.unsqueeze(2).to_broadcast([P, ROWT, E]),
                            iota.unsqueeze(1).to_broadcast([P, ROWT, E]), ALU.is_equal).then_inc(place, 1)
            dve.wait_ge(a_tr, 1)
            V.tensor_copy(a_t, m_wide).then_inc(place, 1)
            V.tensor_copy(a_hl[:, :], m_wide).then_inc(place, 1)
            add_attention(4, 0)
            dve.wait_ge(place, 7)
            V.tensor_tensor(a_hl[PAIRS:P, :], a_t[PAIRS:P, :], a_hl[PAIRS:P, :].bitcast(f32), ALU.subtract)\
                .then_inc(a_ready, 1)

            def row_operands(n, u, turn, first=False):
                rows = bass.ds(RPT * n, RPT)
                if not first:
                    dve.wait_ge(reduced, (RPT // RG) * (n - 1))
                dve.wait_ge(codes_in[u], 16 * turn + 16)
                V.tensor_scalar(pair_hot_t[u].bitcast(f32r), codes_bc[:, u, :], pair_no, None,
                                ALU.is_equal).then_inc(hot_ready, 1)
                V.tensor_copy(row_w_now[:, u, :], row_w[:, rows]).then_inc(roww_ready, 1)
                V.tensor_tensor(pair_w[u], group_hot[:, rows, :].unsqueeze(3).to_broadcast([P, RPT, E, E]),
                                pick_w[:, rows, :].unsqueeze(2).to_broadcast([P, RPT, E, E]),
                                ALU.mult).then_inc(pair_w_ready, 1)

            add_attention(5, 1)
            add_attention(6, 0)
            row_operands(0, 0, 0, first=True)
            add_attention(7, 1)
            row_operands(1, 1, 0, first=True)
            with dve.Fori(0, ROW_TILES // 2 - 1) as b:
                add_attention(FIRST_ROW_TILE + 2 * b, 0)
                row_operands(2 * b + 2, 0, b + 1)
                add_attention(FIRST_ROW_TILE + 2 * b + 1, 1)
                row_operands(2 * b + 3, 1, b + 1)
            dve.wait_ge(rms_ready, NB)
            add_attention(NT - 2, 0)
            add_attention(NT - 1, 1, (0, 1))
            dve.wait_ge(reduced, ROWT // RG)
            V.tensor_copy(a_t, up[2][:, 0:HID]).then_inc(sums_sb, 1)
            dve.wait_ge(sums_tr, 1)
            V.tensor_tensor(sums_b.rearrange("p (r n) -> p r n", r=2), m_wide.rearrange("p (r n) -> p r n", r=2),
                            ab[:, 2, :].unsqueeze(1).to_broadcast([P, 2, PAIRS]), ALU.mult).then_inc(place, 1)
            dve.wait_ge(place, 8)
            V.tensor_tensor(h_sum[:, :], sums_b[:, 0:PAIRS], sums_b[:, PAIRS:P], ALU.add).then_inc(h_pairs, 1)
            add_attention(NT - 1, 1, (2, 3))
            dve.wait_ge(routed, 1)
            for c in range(4):
                cols = slice(c * QTR, (c + 1) * QTR)
                V.tensor_tensor(x_sb[0:E, 0, cols], x_sb[0:E, 0, cols], up[0][32 * c:32 * c + E, 0:QTR], ALU.add)\
                    .then_inc(first8_ready, 1)

        @block.tensor
        def _(pe):
            def parts(w_h, w_l, a_h, a_l):
                return [(w_h, a_h), (w_l, a_h), (w_h, a_l)]

            def first_transposes():
                for t in range(TT):
                    pe.wait_ge(xn_ready, t + 1)
                    for k in range(KC):
                        last = T.transpose(tp[k][:, t * P:(t + 1) * P], xn[:, 0, t, k * P:(k + 1) * P], ident)
                        if t == TT - 1:
                            last.then_inc(tp_ready, 1)

            def transposes(i, u):
                pe.wait_ge(xn_ready, TT * i + TT)
                pe.wait_ge(e_ready, 2 * i)
                for k in range(KC):
                    for t in range(TT):
                        last = T.transpose(tp[k][:, t * P:(t + 1) * P], xn[:, u, t, k * P:(k + 1) * P], ident)
                    last.then_inc(tp_ready, 1)

            def up_half(i, u, m, first=False):
                for n in range(2):
                    if m == 0 and n == 0:
                        if not first:
                            pe.wait_ge(h_ready, 2 * i)
                            pe.wait_ge(gate_sb, i)
                    if m == 1 and n == 1:
                        pe.wait_ge(silu_ready, 2 * i + 1)
                    to = up[(2 * m + n) % 3]
                    cols = slice(n * DIM + m * P, n * DIM + (m + 1) * P)
                    run = [(w[:, k, cols], a[:, u, k, :]) for w, a in parts(wup_h, wup_l, xh, xl) for k in range(KC)]
                    for j, (w, a) in enumerate(run):
                        if first and n == 0:
                            if j < KC:
                                pe.wait_ge(xh_ready, j + 1)
                            elif j == KC:
                                pe.wait_ge(w_lo, 1)
                            elif j >= 2 * KC:
                                pe.wait_ge(xl_ready, j - 2 * KC + 1)
                        elif m == 0 and n == 0 and j == 2 * KC:
                            pe.wait_ge(xl_ready, 2 * i + 2)
                        last = T.matmul(to[:, :], w, a, start=(j == 0), stop=(j == len(run) - 1))
                    last.then_inc(up_ready, 1)

            def gate(i, u):
                pe.wait_ge(h_ready, 2 * i + 1)
                run = [(wg_hl[:, k, :, :].rearrange("p h e -> p (h e)"), a[:, u, k, :])
                       for a in (xh, xl) for k in range(KC)]
                for j, (w, a) in enumerate(run):
                    last = T.matmul(up[1][0:2 * E, :], w, a, start=(j == 0), stop=(j == len(run) - 1))
                last.then_inc(gate_ready, 1)

            def gate_transposes():
                for t in range(TT):
                    last = T.transpose(m_gate[:, 2 * E * t:2 * E * t + 2 * E], gate_rows[:, t * P:(t + 1) * P],
                                       ident[0:2 * E, 0:2 * E])
                last.then_inc(misc_ready, 1)

            def ssq_transpose():
                return T.transpose(m_ssq, ssq_rows, ident)

            def square_sums():
                for t in range(TT):
                    last = T.matmul(m_ssq_rows[32 * t:32 * t + 32, :], ones[:, 0:32], sq[:, 0, t * P:(t + 1) * P],
                                    start=True, stop=True)
                last.then_inc(ssq_ready, 1)

            def wait_down(i, first=False):
                if first:
                    pe.wait_ge(w_lo, 3)
                pe.wait_ge(hl_ready, 2 * i + 2)
                if not first:
                    pe.wait_ge(y_ready, 2 * i)

            def down(u, t):
                tok = slice(t * P, (t + 1) * P)
                run = [(a[:, u, k, tok], w[:, k, :]) for w, a in parts(wdn_h, wdn_l, hh, hl) for k in range(KC)]
                for j, (a, w) in enumerate(run):
                    last = T.matmul(dn[t // 2][:, (t % 2) * DIM:(t % 2 + 1) * DIM], a, w,
                                    start=(j == 0), stop=(j == len(run) - 1))
                if t % 2:
                    last.then_inc(dn_ready, 1)

            def tables():
                pe.wait_ge(w13_in, 64)
                pe.wait_ge(x32_ready, 2)
                for k in range(KC):
                    for c in range(4):
                        w = (w1_sb, w3_sb)[c // 2]
                        last = T.matmul(ab_rows[32 * c:32 * c + 32, :], x32[:, k, :],
                                        w[:, k, 4 * (c % 2):4 * (c % 2) + 4, :].rearrange("p g h -> p (g h)"),
                                        start=(k == 0), stop=(k == KC - 1))
                last.then_inc(ab_ready, 1)

            def tables_transposes():
                for g in range(4):
                    T.transpose(dn[1][:, g * P:(g + 1) * P], ab_rows_sb[:, g * P:(g + 1) * P], ident)

            def batch(b, first=False, last=False):
                for u in range(2):
                    i = 2 * b + u
                    up_half(i, u, 0, first and u == 0)
                    if not (last and u == 1):
                        transposes(i + 1, 1 - u)
                    up_half(i, u, 1)
                    if first and u == 0:
                        tables()
                        pe.wait_ge(w_lo, 2)
                        gate(i, u)
                        pe.wait_ge(ab_sb, 1)
                        tables_transposes()
                        pe.wait_ge(setup, 4)
                        pe.wait_ge(gate_sb, 1)
                        gate_transposes()
                    else:
                        gate_at, transposes_at = (0, 2) if last and u == 1 else (2, TT)
                        for t in range(TT):
                            if t == gate_at:
                                pe.wait_ge(sq_added, i)
                                pe.wait_ge(logit_read, i)
                                if first:
                                    pe.wait_ge(ab_read, 3)
                                else:
                                    pe.wait_ge(ms_read, i - 1)
                                gate(i, u)
                                square_sums()
                            if t == 0:
                                wait_down(i - 1, first)
                            if t == transposes_at - 1:
                                pe.wait_ge(gate_sb, i + 1)
                                pe.wait_ge(ssq_sb, i)
                            down(1 - u, t)
                            if t == transposes_at - 1:
                                ssq_transpose()
                                gate_transposes()

            pe.wait_ge(ones_set, 1)
            for _ in range(CLOCK_PRODUCTS):
                T.matmul(up[2][:, 0:P], ones[:, :], ones[:, :], start=True, stop=True)
            pe.wait_ge(cst_in, 16)
            pe.wait_ge(setup, 1)
            T.matmul(m_wide[:, 0:KC], heads, qk[:, :], start=True, stop=True).then_inc(qk_sum, 1)
            first_transposes()
            batch(0, first=True)
            with pe.Fori(1, NB - 1) as b:
                batch(b)
            batch(NB - 1, last=True)

            def attention(i, u, tiles=range(TT)):
                for t in tiles:
                    if t % 2 == 0:
                        pe.wait_ge(el_ready, 2 * i + t // 2 + 1)
                        if not isinstance(i, int) or i >= 2:
                            pe.wait_ge(o_ready, TT * (i - 2) + t + 2)
                    tok = slice(t * P, (t + 1) * P)
                    run = [(a[:, u, k, tok], w[:, k, :]) for w, a in parts(wo_h, wo_l, xh, xl) for k in range(KC)]
                    for j, (a, w) in enumerate(run):
                        last = T.matmul(att[u][t // 2][:, (t % 2) * DIM:(t % 2 + 1) * DIM], a, w,
                                        start=(j == 0), stop=(j == len(run) - 1))
                    if t % 2:
                        last.then_inc(att_ready, 1)

            pe.wait_ge(w_lo, 4)
            attention(0, 0)
            wait_down(NT - 1)
            for t in range(TT):
                down(1, t)
            pe.wait_ge(y_ready, 2 * NT - 1)
            attention(1, 1, (0, 1))
            pe.wait_ge(y_ready, 2 * NT)
            attention(1, 1, (2, 3))
            pe.wait_ge(ms_read, NT - 1)
            pe.wait_ge(logit_read, NT)
            pe.wait_ge(sq_added, NT)
            square_sums()
            attention(2, 0, (0, 1))
            pe.wait_ge(ssq_sb, NT)
            ssq_transpose().then_inc(misc_ready, 1)
            pe.wait_ge(ms_read, NT)
            pe.wait_ge(place, 1)
            T.matmul(m_wide[:, 0:E], ones[:, :], count[:, :], start=True, stop=True).then_inc(count_ready, 1)
            attention(2, 0, (2, 3))
            attention(3, 1)
            attention(4, 0, (0, 1))
            pe.wait_ge(code_ready, 1)
            T.transpose(m_wide, code, ident).then_inc(code_tr, 1)
            attention(4, 0, (2, 3))
            pe.wait_ge(code_sb, 1)
            T.transpose(m_wide, ab[:, 0:2, :].rearrange("p a c -> p (a c)"), ident).then_inc(a_tr, 1)
            for i in range(5, FIRST_ROW_TILE):
                attention(i, i % 2)

            def gather(n, u, q):
                for r in range(RG):
                    j = RG * q + r
                    last = T.matmul(up[q % 2][:, r * HID:(r + 1) * HID],
                                    pair_hot_t[u][:, j * P:(j + 1) * P], a_hl[:, :], start=True, stop=True)
                last.then_inc(gathered, 1)

            def reduce(n, u, q, last=False):
                pe.wait_ge(row_silu, RPT * n + RG * (q + 1))
                for r in range(RG):
                    j = RG * q + r
                    to = PAIRS * (r % 2)
                    done = T.matmul(up[2][to:to + PAIRS, 0:HID], pair_w[u][:, j, :, :].rearrange("p g e -> p (g e)"),
                                    act_out[:, q % 2, r * HID:(r + 1) * HID],
                                    start=False, stop=(last and r >= RG - 2))
                done.then_inc(reduced, 1)

            def row_tile(n, u, last=False):
                i = FIRST_ROW_TILE + n
                banks = RPT // RG
                attention(i, u, (0,))
                pe.wait_ge(pair_w_ready, n + 1)
                for q in range(banks):
                    reduce(n, u, q, last and q == banks - 1)
                    if q + 2 < banks:
                        gather(n, u, q + 2)
                    elif not last:
                        if q + 2 == banks:
                            pe.wait_ge(hot_ready, n + 2)
                        gather(n + 1, 1 - u, q + 2 - banks)
                    if q + 1 < (TT - 1 if last else TT):
                        attention(i, u, (q + 1,))
                if last:
                    pe.wait_ge(sums_sb, 1)
                    attention(i, u, (TT - 1,))
                    T.transpose(m_wide, a_t, ident).then_inc(sums_tr, 1)

            pe.wait_ge(zeros_set, 1)
            T.matmul(up[2][:, 0:HID].rearrange("p (r n) -> p r n", r=2), ones[:, :],
                     h_sum[:, :].unsqueeze(1).to_broadcast([P, 2, PAIRS]), start=True, stop=False)
            pe.wait_ge(a_ready, 1)
            pe.wait_ge(hot_ready, 1)
            gather(0, 0, 0)
            gather(0, 0, 1)
            with pe.Fori(0, ROW_TILES // 2 - 1) as b:
                row_tile(2 * b, 0)
                row_tile(2 * b + 1, 1)
            row_tile(ROW_TILES - 2, 0)
            row_tile(ROW_TILES - 1, 1, last=True)
            pe.wait_ge(w2_in, 16)
            pe.wait_ge(h_pairs, 1)
            for g in range(E):
                for c in range(4):
                    last = T.matmul(up[0][32 * c:32 * c + E, 0:QTR], h_sum[:, E * g:E * g + E],
                                    w2_sb[:, g, c * QTR:(c + 1) * QTR], start=(g == 0), stop=(g == E - 1))
            last.then_inc(routed, 1)


def constants():
    import numpy as np

    c = np.zeros((P, C_END), np.float32)
    p = np.arange(P)
    c[:, C_IDENT:C_IDENT + P] = np.eye(P)
    c[:, C_HEADS:C_HEADS + P] = (p[:, None] // 16 == p[None, :] // 16)
    for col, n in ((C_THR8, E), (C_THR4, GRP)):
        j, i = np.divmod(np.arange(n * n), n)
        c[:, col:col + n * n] = np.where(i < j, 0.0, LEAST)[None, :]
    j = np.arange(ROWT)
    c[:, C_POS:C_POS + ROWT] = 2 * P * (j // 2)[None, :] + 2 * p[:, None] + (j % 2)[None, :]
    c[:, C_IOTA:C_IOTA + E] = np.arange(E)
    c[:, C_PAIR] = p % PAIRS
    return c


def kernel(L0_attn_x, L0_attn_q, L0_attn_k, L0_attn_log_decay, L0_attn_norm_weight, L0_attn_o_w,
           L0_ffn_w_gate, L0_ffn_w1, L0_ffn_w2, L0_ffn_w3, L0_ffn_sw1, L0_ffn_sw2, L0_ffn_sw3,
           L0_ffn_expert_bias):
    import numpy as np
    import concourse.bacc as bacc
    from concourse.bass_utils import run_bass_kernel_spmd

    x = np.asarray(L0_attn_x)
    small = np.zeros((P, S_END), np.float32)

    def columns(v):
        return np.asarray(v).reshape(KC, P).T

    small[:, S_Q:S_Q + KC] = columns(L0_attn_q)
    small[:, S_K:S_K + KC] = columns(L0_attn_k)
    small[:, S_NW:S_NW + KC] = columns(L0_attn_norm_weight)
    small[:, S_LD:S_LD + KC] = columns(np.repeat(np.asarray(L0_attn_log_decay), DIM // 16))
    small[:, S_EB:S_END] = np.asarray(L0_ffn_expert_bias)[None, :]
    arrays = {
        "x": x.reshape(TOKENS, DIM),
        "small": small,
        "w_gate": np.asarray(L0_ffn_w_gate).T,
        "w_up": np.concatenate([np.asarray(L0_ffn_sw1).T, np.asarray(L0_ffn_sw3).T], axis=1),
        "w_down": np.asarray(L0_ffn_sw2).T,
        "w_o": np.asarray(L0_attn_o_w).T,
        "w1": np.asarray(L0_ffn_w1),
        "w2": np.asarray(L0_ffn_w2),
        "w3": np.asarray(L0_ffn_w3),
        "consts": constants(),
    }
    arrays = {n: np.ascontiguousarray(a) for n, a in arrays.items()}
    nc = bacc.Bacc("TRN2", target_bir_lowering=False, num_devices=1)
    args = [nc.dram_tensor(n, a.shape, mybir.dt.from_np(a.dtype), kind="ExternalInput").ap()
            for n, a in arrays.items()]
    out = nc.dram_tensor("out", (TOKENS, DIM), mybir.dt.float32, kind="ExternalOutput").ap()
    build(nc, *args, out)
    got = run_bass_kernel_spmd(nc, [arrays], core_ids=[0])
    return got.results[0]["out"].reshape(x.shape)
```
